# Optimizing a Trainium2 kernel written in Bass

```python
import numpy as np
import jax
import jax.numpy as jnp

def _softmax(x, axis=-1):
    return jax.nn.softmax(x, axis=axis)

def _gelu(x):
    return jax.nn.gelu(x, approximate=True)

def _silu(x):
    return jax.nn.silu(x)

def _sigmoid(x):
    return jax.nn.sigmoid(x)

def _layernorm(x, axis=-1, eps=1e-05):
    m = jnp.mean(x, axis=axis, keepdims=True)
    v = jnp.var(x, axis=axis, keepdims=True)
    return (x - m) / jnp.sqrt(v + eps)

def _scatter_add(tgt, idx, src, axis=0):
    return tgt.at[idx].add(src)

def _segment_sum(src, seg, n):
    return jax.ops.segment_sum(src, seg, n)
kernel_name = 'mk_cond_resid_d4_seqx_r4_ff8993'

def setup_inputs(seed: int=0):
    np.random.seed(seed)
    _w = jnp.asarray

    def _rec_inputs():
        import jax
        import jax.numpy as jnp
        _rk = jax.random.key(seed)
        x = -0.000125 + 0.9999 * jax.random.normal(jax.random.fold_in(_rk, 1), (4, 512, 256), jnp.float32)
        _lenS = 512 - jax.random.randint(jax.random.fold_in(_rk, 7), (4,), 0, max(1, 512 // 4) + 1, jnp.int32)
        _lenS2 = 512 - jax.random.randint(jax.random.fold_in(_rk, 8), (4,), 0, max(1, 512 // 4) + 1, jnp.int32)
        cond_512 = 0.0061147 + 1.02565 * jax.random.normal(jax.random.fold_in(_rk, 11), (4, 128), jnp.float32)
        return (x, cond_512)
    x, cond_512 = _rec_inputs()

    def _L0_cond_setup():
        import jax, jax.numpy as jnp
        import numpy as np
        B, S, D, H, C = (8, 1024, 256, 64, 128)
        INIT_RANGE = 0.01
        key = jax.random.key(seed)
        ks = jax.random.split(key, 6)
        return {'hidden_states': jax.random.normal(ks[0], (B, S, D), dtype=jnp.float32), 'conditions': jax.random.normal(ks[1], (B, C), dtype=jnp.float32), 'down_project': jax.random.normal(ks[2], (D, H), dtype=jnp.float32) * INIT_RANGE, 'down_gamma': jax.random.normal(ks[3], (C, H), dtype=jnp.float32), 'down_beta': jnp.zeros((C, H), dtype=jnp.float32), 'up_project': jax.random.normal(ks[4], (H, D), dtype=jnp.float32) * INIT_RANGE, 'up_gamma': jax.random.normal(ks[5], (C, D), dtype=jnp.float32), 'up_beta': jnp.zeros((C, D), dtype=jnp.float32)}
    _L0_cond_all = _L0_cond_setup()
    _L0_cond_in = {k: v for k, v in _L0_cond_all.items() if k in ('down_project', 'down_gamma', 'down_beta', 'up_project', 'up_gamma', 'up_beta')}
    del _L0_cond_all

    def _L1_cond_setup():
        import jax, jax.numpy as jnp
        import numpy as np
        W_DIM = 128
        CLAMP = 256.0
        key = jax.random.key(seed)
        ks = jax.random.split(key, 6)
        B, L, C = (8, 2048, 256)
        return {'x': jax.random.normal(ks[0], (B, L, C), dtype=jnp.float32), 'w': jax.random.normal(ks[1], (B, W_DIM), dtype=jnp.float32), 'weight': jax.random.normal(ks[2], (C, C), dtype=jnp.float32), 'bias': jax.random.normal(ks[3], (C,), dtype=jnp.float32), 'affine_w': jax.random.normal(ks[4], (C, W_DIM), dtype=jnp.float32), 'affine_b': jnp.ones((C,), dtype=jnp.float32)}
    _L1_cond_all = _L1_cond_setup()
    _L1_cond_in = {k: v for k, v in _L1_cond_all.items() if k in ('weight', 'bias', 'affine_w', 'affine_b')}
    del _L1_cond_all

    def _L2_cond_setup():
        import jax, jax.numpy as jnp
        import numpy as np
        import math
        HEAD_NUM = 16
        EPS = 1e-08

        def modulated_linear(x, s, aff_w, aff_b, w, b):
            style = s @ aff_w.T + aff_b
            w_mod = w[None, :, :] * style[:, None, :]
            demod = jax.lax.rsqrt(jnp.sum(w_mod * w_mod, axis=2) + EPS)
            w_mod = w_mod * demod[:, :, None]
            return jnp.einsum('bni,boi->bno', x, w_mod) + b
        key = jax.random.key(seed)
        ks = jax.random.split(key, 6)
        B, N, F, S = (8, 256, 256, 128)
        return {'x': jax.random.normal(ks[0], (B, N, F), dtype=jnp.float32), 's': jax.random.normal(ks[1], (B, S), dtype=jnp.float32), 'k_aff_w': jax.random.normal(ks[2], (F, S), dtype=jnp.float32) * 0.02, 'k_aff_b': jnp.ones((F,), dtype=jnp.float32), 'k_w': jax.random.normal(ks[3], (F, F), dtype=jnp.float32) * 0.02, 'k_b': jnp.zeros((F,), dtype=jnp.float32), 'o_aff_w': jax.random.normal(ks[4], (F, S), dtype=jnp.float32) * 0.02, 'o_aff_b': jnp.ones((F,), dtype=jnp.float32), 'o_w': jax.random.normal(ks[5], (F, F), dtype=jnp.float32) * 0.02, 'o_b': jnp.zeros((F,), dtype=jnp.float32)}
    _L2_cond_all = _L2_cond_setup()
    _L2_cond_in = {k: v for k, v in _L2_cond_all.items() if k in ('k_aff_w', 'k_aff_b', 'k_w', 'k_b', 'o_aff_w', 'o_aff_b', 'o_w', 'o_b')}
    del _L2_cond_all

    def _L3_cond_setup():
        import jax, jax.numpy as jnp
        import numpy as np
        IN_DIM = 256
        OUT_DIM = 256
        MU_DIM = 128
        K = 30
        key = jax.random.key(seed)
        k1, k2, k3, k4, k5 = jax.random.split(key, 5)
        B, S = (16, 512)
        x = jax.random.normal(k1, (B, S, IN_DIM), dtype=jnp.float32)
        mu = jax.random.normal(k2, (B, MU_DIM), dtype=jnp.float32)
        W_dec = jax.random.normal(k3, (MU_DIM, (IN_DIM + 1) * K), dtype=jnp.float32) / np.sqrt(MU_DIM)
        b_dec = jax.random.normal(k4, ((IN_DIM + 1) * K,), dtype=jnp.float32) * 0.01
        V = jax.random.normal(k5, (K, OUT_DIM), dtype=jnp.float32) / np.sqrt(K)
        return {'x': x, 'mu': mu, 'W_dec': W_dec, 'b_dec': b_dec, 'V': V}
    _L3_cond_all = _L3_cond_setup()
    _L3_cond_in = {k: v for k, v in _L3_cond_all.items() if k in ('W_dec', 'b_dec', 'V')}
    del _L3_cond_all
    return {'x': x, 'cond_512': cond_512, 'L0_cond_down_project': _L0_cond_in['down_project'], 'L0_cond_down_gamma': _L0_cond_in['down_gamma'], 'L0_cond_down_beta': _L0_cond_in['down_beta'], 'L0_cond_up_project': _L0_cond_in['up_project'], 'L0_cond_up_gamma': _L0_cond_in['up_gamma'], 'L0_cond_up_beta': _L0_cond_in['up_beta'], 'L1_cond_weight': _L1_cond_in['weight'], 'L1_cond_bias': _L1_cond_in['bias'], 'L1_cond_affine_w': _L1_cond_in['affine_w'], 'L1_cond_affine_b': _L1_cond_in['affine_b'], 'L2_cond_k_aff_w': _L2_cond_in['k_aff_w'], 'L2_cond_k_aff_b': _L2_cond_in['k_aff_b'], 'L2_cond_k_w': _L2_cond_in['k_w'], 'L2_cond_k_b': _L2_cond_in['k_b'], 'L2_cond_o_aff_w': _L2_cond_in['o_aff_w'], 'L2_cond_o_aff_b': _L2_cond_in['o_aff_b'], 'L2_cond_o_w': _L2_cond_in['o_w'], 'L2_cond_o_b': _L2_cond_in['o_b'], 'L3_cond_W_dec': _L3_cond_in['W_dec'], 'L3_cond_b_dec': _L3_cond_in['b_dec'], 'L3_cond_V': _L3_cond_in['V']}

def reference(x, cond_512, L0_cond_down_project, L0_cond_down_gamma, L0_cond_down_beta, L0_cond_up_project, L0_cond_up_gamma, L0_cond_up_beta, L1_cond_weight, L1_cond_bias, L1_cond_affine_w, L1_cond_affine_b, L2_cond_k_aff_w, L2_cond_k_aff_b, L2_cond_k_w, L2_cond_k_b, L2_cond_o_aff_w, L2_cond_o_aff_b, L2_cond_o_w, L2_cond_o_b, L3_cond_W_dec, L3_cond_b_dec, L3_cond_V):
    import jax
    import jax.numpy as jnp

    def _L0_cond_ref(hidden_states, conditions, down_project, down_gamma, down_beta, up_project, up_gamma, up_beta):
        import jax, jax.numpy as jnp
        import numpy as np
        B, S, D, H, C = (8, 1024, 256, 64, 128)
        INIT_RANGE = 0.01
        dg = conditions @ down_gamma
        db = conditions @ down_beta
        ug = conditions @ up_gamma
        ub = conditions @ up_beta
        w_down = down_project[None, :, :] * dg[:, None, :] + db[:, None, :]
        down = jnp.einsum('bsd,bdh->bsh', hidden_states, w_down)
        act = jax.nn.relu(down)
        w_up = up_project[None, :, :] * ug[:, None, :] + ub[:, None, :]
        up = jnp.einsum('bsh,bhd->bsd', act, w_up)
        return up + hidden_states

    def _L1_cond_ref(x, w, weight, bias, affine_w, affine_b):
        import jax, jax.numpy as jnp
        import numpy as np
        W_DIM = 128
        CLAMP = 256.0
        B, L, C = x.shape
        gain = 1.0 / np.sqrt(W_DIM).astype(np.float32)
        styles = w @ (affine_w * gain).T + affine_b
        ws = weight[None, :, :] * styles[:, None, :]
        dcoefs = jax.lax.rsqrt(jnp.sum(ws * ws, axis=2) + 1e-08)
        xm = x * styles[:, None, :]
        y = jnp.einsum('blc,oc->blo', xm, weight)
        y = y * dcoefs[:, None, :]
        y = jnp.clip(y + bias, -CLAMP, CLAMP)
        return y

    def _L2_cond_ref(x, s, k_aff_w, k_aff_b, k_w, k_b, o_aff_w, o_aff_b, o_w, o_b):
        import jax, jax.numpy as jnp
        import numpy as np
        import math
        HEAD_NUM = 16
        EPS = 1e-08

        def modulated_linear(x, s, aff_w, aff_b, w, b):
            style = s @ aff_w.T + aff_b
            w_mod = w[None, :, :] * style[:, None, :]
            demod = jax.lax.rsqrt(jnp.sum(w_mod * w_mod, axis=2) + EPS)
            w_mod = w_mod * demod[:, :, None]
            return jnp.einsum('bni,boi->bno', x, w_mod) + b
        B, N, F = x.shape
        H = HEAD_NUM
        D = F // H
        kx = modulated_linear(x, s, k_aff_w, k_aff_b, k_w, k_b)
        kx = kx.reshape(B, N, H, D)
        q = k = v = kx
        scores = jnp.einsum('bnhd,bnjd->bnhj', q, k) / math.sqrt(D)
        A = jax.nn.softmax(scores, axis=-1)
        out = jnp.einsum('bnhj,bnjd->bnhd', A, v).reshape(B, N, F)
        out = modulated_linear(out, s, o_aff_w, o_aff_b, o_w, o_b)
        return out

    def _L3_cond_ref(x, mu, W_dec, b_dec, V):
        import jax, jax.numpy as jnp
        import numpy as np
        IN_DIM = 256
        OUT_DIM = 256
        MU_DIM = 128
        K = 30
        B = mu.shape[0]
        U = (mu @ W_dec + b_dec).reshape(B, IN_DIM + 1, K)
        param = jnp.einsum('bik,kj->bij', U, V)
        weight = param[:, :-1, :]
        bias = param[:, -1, :]
        out = jnp.einsum('bsd,bde->bse', x, weight)
        out = out + bias[:, None, :]
        return out
    x = x + _L0_cond_ref(x, cond_512, L0_cond_down_project, L0_cond_down_gamma, L0_cond_down_beta, L0_cond_up_project, L0_cond_up_gamma, L0_cond_up_beta)
    x = x + _L1_cond_ref(x, cond_512, L1_cond_weight, L1_cond_bias, L1_cond_affine_w, L1_cond_affine_b)
    x = x + _L2_cond_ref(x, cond_512, L2_cond_k_aff_w, L2_cond_k_aff_b, L2_cond_k_w, L2_cond_k_b, L2_cond_o_aff_w, L2_cond_o_aff_b, L2_cond_o_w, L2_cond_o_b)
    x = x + _L3_cond_ref(x, cond_512, L3_cond_W_dec, L3_cond_b_dec, L3_cond_V)
    return x

_drawn_inputs = setup_inputs


def setup_inputs(seed=0):
    import zlib

    import numpy as np

    out = dict(_drawn_inputs(seed))
    spreads = {'L0_cond_down_beta': (0.0, 0.1),
     'L0_cond_up_beta': (0.0, 0.1),
     'L1_cond_affine_b': (1.0, 0.2),
     'L2_cond_k_aff_b': (1.0, 0.2),
     'L2_cond_k_b': (0.0, 2.0),
     'L2_cond_o_aff_b': (1.0, 0.2),
     'L2_cond_o_b': (0.0, 2.0)}
    factors = {'L1_cond_bias': 29.354, 'L3_cond_b_dec': 6.616}
    for name, (base, spread) in spreads.items():
        noise = np.random.default_rng([zlib.crc32(name.encode()), seed]).standard_normal(out[name].shape)
        drawn = base * np.exp(spread * noise) if base else spread * noise
        out[name] = jnp.asarray(drawn.astype(out[name].dtype))
    for name, factor in factors.items():
        out[name] = (out[name] * factor).astype(out[name].dtype)
    return out
```

```python
import numpy as np

import concourse.bass as bass
from concourse import mybir

B, S, D, C = 4, 512, 256, 128
HID = 64
NH, HD = 16, 16
RANK = 30
P = 128
NC_ = D // P
TILES = 2
TOK = S // TILES
U = 2
STRIP = 32
G = P // STRIP
PL = STRIP // 2
MOD = 3
CHUNK = 2 * D
NCH = RANK // 2
GAIN = float(1.0 / np.sqrt(C).astype(np.float32))
EPS = 1e-8
CLAMP = 256.0

PAR = {}
_at = 0
for _n, _w in (("cond", B), ("affb", MOD * NC_), ("outb", 2 * NC_), ("aff", MOD * D),
               ("down", NC_ * HID), ("gbdown", 2 * HID), ("gbup", 2 * D), ("up", D)):
    PAR[_n] = slice(_at, _at + _w)
    _at += _w
PARW = _at
CONSTW = 3 * P + U


def cond_resid_kernel(nc, xT, params, weights, kb, wdec, wdecb, bdec, vmat, consts, outT):
    f32 = mybir.dt.float32
    ALU = mybir.AluOpType
    ACT = mybir.ActivationFunctionType
    AX = mybir.AxisListType
    from contextlib import ExitStack

    ctx = ExitStack()
    with ctx:
        def sb(name, shape):
            return ctx.enter_context(nc.sbuf_tensor(name, shape, f32))

        def sem(name):
            return ctx.enter_context(nc.semaphore(name))

        par = sb("par", [P, PARW])
        w_raw = sb("w_raw", [P, MOD, NC_, D])
        w_sq = sb("w_sq", [P, MOD, NC_, D])
        kb_b = sb("kb_b", [P, NH, HD])
        wdec_sb = sb("wdec_sb", [P, RANK, D])
        wdecb_sb = sb("wdecb_sb", [P, RANK])
        bdec_sb = sb("bdec_sb", [RANK, D + 1])
        v_sb = sb("v_sb", [RANK, D])
        con = sb("con", [P, CONSTW])
        x_sb = sb("x_sb", [P, B, NC_, S])
        cond_b = sb("cond_b", [P, B, P])
        cond_z = sb("cond_z", [P, STRIP])
        style = sb("style", [P, MOD, NC_, B])
        style_sq = sb("style_sq", [P, MOD, NC_, B])
        ksq_b = sb("ksq_b", [P, NC_, B, P])
        var = sb("var", [P, B * D + 2 * NC_ * B])
        root = sb("root", [P, B * D + 2 * NC_ * B])
        dem = sb("dem", [P, B * D + 2 * NC_ * B])
        dem_k = dem[:, 0:B * D].rearrange("p (b o) -> p b o", b=B)
        dem_1o = dem[:, B * D:].rearrange("p (l c b) -> p l c b", l=2, c=NC_)
        gb_down = sb("gb_down", [P, B, 2, HID])
        gb_up = sb("gb_up", [HID, B, 2, D])
        urow = sb("urow", [P, 4, 2, D])
        u_sb = sb("u_sb", [RANK, B, D])
        ub_sb = sb("ub_sb", [RANK, B])
        bias3 = sb("bias3", [P, NC_, B])
        w_down = sb("w_down", [P, NC_, HID])
        w_up = sb("w_up", [HID, D])
        w_l1 = sb("w_l1", [P, NC_, D])
        w_k = sb("w_k", [P, NC_, D])
        w_o = sb("w_o", [P, NC_, D])
        w_3 = sb("w_3", [P, NC_, D])
        hid = sb("hid", [HID, S])
        x0 = sb("x0", [P, NC_, S])
        y1 = sb("y1", [P, NC_, S])
        x1 = sb("x1", [P, NC_, S])
        x1b = sb("x1b", [P, NC_, S])
        x2 = sb("x2", [P, NC_, S])
        att = sb("att", [P, NC_, S])
        res = sb("res", [P, NC_, S])
        kx = [sb(f"kx{t}", [P, U, NH, HD]) for t in range(TILES)]
        kT = [sb(f"kT{t}", [P, NH, STRIP]) for t in range(TILES)]
        kTz = [sb(f"kTz{t}", [P, U, NH, STRIP]) for t in range(TILES)]
        vT = [sb(f"vT{t}", [P, HD, STRIP]) for t in range(TILES)]
        sc = sb("sc", [P, U * NH, STRIP])
        mx = sb("mx", [P, U * NH])
        sh = sb("sh", [P, U * NH, NH])
        ex = sb("ex", [P, U * NH, NH])
        zs = sb("zs", [P, U * NH])
        rz = sb("rz", [P, U * NH])
        pn = sb("pn", [P, U * NH, NH])
        pT = sb("pT", [P, NH, STRIP])
        pTz = [sb(f"pTz{t}", [P, U, NH, STRIP]) for t in range(TILES)]
        ot = [sb(f"ot{t}", [P, U, STRIP, NH]) for t in range(TILES)]

        urow_d = nc.dram_tensor("urow_d", [B, 4, G, 2, D], f32, kind="Internal").ap()

        ps_s = ctx.enter_context(nc.psum_tensor("ps_s", [P, 2, U * NH, PL], f32))
        ps_o = ctx.enter_context(nc.psum_tensor("ps_o", [P, 2, U * HD, PL], f32))
        ps_p = ctx.enter_context(nc.psum_tensor("ps_p", [P, 2, S], f32))
        ps_q = ctx.enter_context(nc.psum_tensor("ps_q", [P, 2, S], f32))

        ident = con[:, P:2 * P]
        half = [con[:, 3 * P + u:3 * P + u + 1] for u in range(U)]
        cond = par[:, PAR["cond"]]
        affb = par[:, PAR["affb"]]
        outb = par[:, PAR["outb"]]
        aff = par[:, PAR["aff"]].rearrange("p (l i) -> p l i", l=MOD)
        wd_raw = par[:, PAR["down"]].rearrange("p (c h) -> p c h", c=NC_)
        gbd_raw = par[:, PAR["gbdown"]]
        gbu_raw = par[:, PAR["gbup"]]
        wu_raw = par[0:HID, PAR["up"]]

        S_par_in = sem("par_in")
        S_w_in = sem("w_in")
        S_kb_in = sem("kb_in")
        S_con_in = sem("con_in")
        S_dec_in = sem("dec_in")
        S_x_in = sem("x_in")
        S_out_dma = sem("out_dma")
        S_ur_out = sem("ur_out")
        S_ur_in = sem("ur_in")
        S_ones_in = sem("ones_in")
        S_zeroed = sem("zeroed")
        S_conds = sem("conds")
        S_style_ps = sem("style_ps")
        S_styled = sem("styled")
        S_squares = sem("squares")
        S_style_sqs = sem("style_sqs")
        S_var_ps = sem("var_ps")
        S_vars = sem("vars")
        S_roots = sem("roots")
        S_dems = sem("dems")
        S_newton = sem("newton")
        S_gbd_ps = sem("gbd_ps")
        S_gbd = sem("gbd")
        S_gbu_ps = sem("gbu_ps")
        S_gbu = sem("gbu")
        S_urow_ps = sem("urow_ps")
        S_urow_sb = sem("urow_sb")
        S_u_added = sem("u_added")
        S_ub_added = sem("ub_added")
        S_ub_ps = sem("ub_ps")
        S_b3_ps = sem("b3_ps")
        S_b3 = sem("b3")
        S_wdown_rdy = sem("wdown_rdy")
        S_wup_rdy = sem("wup_rdy")
        S_wl1_rdy = sem("wl1_rdy")
        S_wk_rdy = sem("wk_rdy")
        S_wo_rdy = sem("wo_rdy")
        S_w3_ps = sem("w3_ps")
        S_w3_rdy = sem("w3_rdy")
        S_wdown_scaled = sem("wdown_scaled")
        S_wup_scaled = sem("wup_scaled")
        S_wk_scaled = sem("wk_scaled")
        S_down_ps = sem("down_ps")
        S_hid_rdy = sem("hid_rdy")
        S_up_ps = sem("up_ps")
        S_x0_rdy = sem("x0_rdy")
        S_l1_ps = sem("l1_ps")
        S_y_rdy = sem("y_rdy")
        S_clipped = sem("clipped")
        S_x1_rdy = sem("x1_rdy")
        S_x1b_rdy = sem("x1b_rdy")
        S_k_ps = sem("k_ps")
        S_kx_rdy = sem("kx_rdy")
        S_kT_rdy = sem("kT_rdy")
        S_kTz_rdy = sem("kTz_rdy")
        S_vT_rdy = sem("vT_rdy")
        S_s_ps = sem("s_ps")
        S_sc_rdy = sem("sc_rdy")
        S_mx_rdy = sem("mx_rdy")
        S_sh_rdy = sem("sh_rdy")
        S_ex_rdy = sem("ex_rdy")
        S_zs_rdy = sem("zs_rdy")
        S_rz_rdy = sem("rz_rdy")
        S_pn_rdy = sem("pn_rdy")
        S_pT_rdy = sem("pT_rdy")
        S_pTz_rdy = sem("pTz_rdy")
        S_o_ps = sem("o_ps")
        S_ot_rdy = sem("ot_rdy")
        S_tr_ps = sem("tr_ps")
        S_att_rdy = sem("att_rdy")
        S_op_ps = sem("op_ps")
        S_x2_rdy = sem("x2_rdy")
        S_l3_ps = sem("l3_ps")
        S_res_rdy = sem("res_rdy")

        block = ctx.enter_context(nc.Block())

        @block.sync
        def _(sp):
            sp.dma_start(par[:], params).then_inc(S_par_in, 16)
            sp.dma_start(x_sb[:, 0], xT[:, 0]).then_inc(S_x_in, 16)
            sp.dma_start(wdec_sb[:], wdec).then_inc(S_dec_in, 16)
            sp.dma_start(wdecb_sb[:], wdecb).then_inc(S_dec_in, 16)
            sp.dma_start(bdec_sb[:], bdec).then_inc(S_dec_in, 16)
            sp.dma_start(v_sb[:], vmat).then_inc(S_dec_in, 16)
            for b in range(1, B):
                sp.wait_ge(S_x_in, 16 * b)
                sp.dma_start(x_sb[:, b], xT[:, b]).then_inc(S_x_in, 16)
            sp.wait_ge(S_urow_sb, 4)
            for g in range(G):
                slots = 4 if 3 * G + g < NCH else 3
                sp.dma_start(urow_d[:, 0:slots, g], urow[STRIP * g:STRIP * g + B, 0:slots]).then_inc(S_ur_out, 16)
            sp.wait_ge(S_ur_out, 16 * G)
            sp.dma_start(u_sb[:], urow_d.rearrange("b n g k i -> (n g k) b i")[0:RANK]).then_inc(S_ur_in, 16)

            for b in range(B):
                sp.wait_ge(S_res_rdy, 2 * b + 2)
                sp.dma_start(outT[:, b], res[:]).then_inc(S_out_dma, 16)
            sp.wait_ge(S_out_dma, 16 * B)

        @block.gpsimd
        def _(pool):
            def weights_down_up(b):
                pool.wait_ge(S_gbd, 1)
                pool.wait_ge(S_down_ps, b)
                gd = gb_down[:, b, 0:1].to_broadcast([P, NC_, HID])
                bd = gb_down[:, b, 1:2].to_broadcast([P, NC_, HID])
                pool.tensor_tensor(w_down[:], wd_raw, gd, ALU.mult).then_inc(S_wdown_scaled, 1)
                pool.wait_ge(S_wdown_scaled, b + 1)
                pool.tensor_tensor(w_down[:], w_down[:], bd, ALU.add).then_inc(S_wdown_rdy, 1)
                pool.wait_ge(S_gbu, b + 1)
                pool.wait_ge(S_up_ps, 2 * b)
                pool.tensor_tensor(w_up[:], wu_raw, gb_up[:, b, 0], ALU.mult).then_inc(S_wup_scaled, 1)
                pool.wait_ge(S_wup_scaled, b + 1)
                pool.tensor_tensor(w_up[:], w_up[:], gb_up[:, b, 1], ALU.add).then_inc(S_wup_rdy, 1)

            def weights_l1_k(b):
                pool.wait_ge(S_styled, 6)
                pool.wait_ge(S_l1_ps, 2 * b)
                for c in range(NC_):
                    pool.tensor_scalar(w_l1[:, c], w_raw[:, 0, c], style[:, 0, c, b:b + 1], 1.0,
                                       ALU.mult, ALU.mult).then_inc(S_wl1_rdy, 1)
                pool.wait_ge(S_k_ps, 2 * b)
                pool.wait_ge(S_newton, 1)
                for c in range(NC_):
                    pool.tensor_scalar(w_k[:, c], w_raw[:, 1, c], style[:, 1, c, b:b + 1], 1.0,
                                       ALU.mult, ALU.mult).then_inc(S_wk_scaled, 1)
                for c in range(NC_):
                    pool.wait_ge(S_wk_scaled, 2 * b + c + 1)
                    pool.tensor_tensor(w_k[:, c], w_k[:, c], dem_k[:, b], ALU.mult).then_inc(S_wk_rdy, 1)

            def weights_o(b):
                pool.wait_ge(S_op_ps, 2 * b)
                for c in range(NC_):
                    pool.tensor_scalar(w_o[:, c], w_raw[:, 2, c], style[:, 2, c, b:b + 1], 1.0,
                                       ALU.mult, ALU.mult).then_inc(S_wo_rdy, 1)

            def residual_bias(b):
                pool.wait_ge(S_x1_rdy, 2 * b + 2)
                pool.wait_ge(S_x2_rdy, 2 * b)
                for c in range(NC_):
                    pool.tensor_scalar(x1b[:, c], x1[:, c], outb[:, NC_ + c:NC_ + c + 1], 0.0,
                                       ALU.add, ALU.add).then_inc(S_x1b_rdy, 1)

            pool.wait_ge(S_par_in, 16)
            pool.wait_ge(S_w_in, 16)
            weights_down_up(0)
            weights_l1_k(0)
            pool.wait_ge(S_dec_in, 64)
            residual_bias(0)
            pool.wait_ge(S_ur_in, 16)
            pool.tensor_tensor(u_sb[:], u_sb[:], bdec_sb[:, 0:D].rearrange("k (o i) -> k o i", o=1).to_broadcast([RANK, B, D]),
                               ALU.add).then_inc(S_u_added, 1)

            def batch(b, nxt):
                if nxt:
                    weights_down_up(b + 1)
                    weights_l1_k(b + 1)
                weights_o(b)
                if nxt:
                    residual_bias(b + 1)

            for b in range(B):
                batch(b, b + 1 < B)

        @block.scalar
        def _(act):
            act.dma_start(con[:], consts).then_inc(S_con_in, 16)
            act.dma_start(w_raw[:], weights).then_inc(S_w_in, 16)
            act.dma_start(kb_b[:], kb.to_broadcast([P, D]).rearrange("p (h d) -> p h d", h=NH)).then_inc(S_kb_in, 16)
            act.wait_ge(S_w_in, 16)
            nc.scalar.activation(w_sq[:], w_raw[:], ACT.Square).then_inc(S_squares, 1)
            for b in range(B):
                act.wait_ge(S_gbu_ps, b + 1)
                nc.scalar.activation(gb_up[:, b], ps_q[0:HID, b % 2].rearrange("h (g i) -> h g i", g=2), ACT.Copy).then_inc(S_gbu, 1)
            act.wait_ge(S_vars, 2)
            nc.scalar.activation(root[:], var[:], ACT.Sqrt).then_inc(S_roots, 1)

            def relu(b):
                act.wait_ge(S_down_ps, b + 1)
                act.wait_ge(S_up_ps, 2 * b)
                nc.scalar.activation(hid[:], ps_q[0:HID, 0], ACT.Relu).then_inc(S_hid_rdy, 1)

            def demodulate(b):
                for c in range(NC_):
                    act.wait_ge(S_l1_ps, 2 * b + c + 1)
                    act.wait_ge(S_x1_rdy, 2 * b)
                    nc.scalar.activation(y1[:, c], ps_q[:, c], ACT.Identity, bias=outb[:, c:c + 1],
                                         scale=dem_1o[:, 0, c, b:b + 1]).then_inc(S_y_rdy, 1)

            def exponentials(b, t):
                act.wait_ge(S_sh_rdy, 2 * b + t + 1)
                act.wait_ge(S_pn_rdy, 2 * b + t)
                nc.scalar.activation(ex[:], sh[:], ACT.Exp, scale=HD ** -0.5).then_inc(S_ex_rdy, 1)

            def attention_copy(b):
                act.wait_ge(S_op_ps, 2 * b)
                for c in range(NC_):
                    act.wait_ge(S_tr_ps, 2 * b + c + 1)
                    nc.scalar.activation(att[:, c], ps_q[:, c], ACT.Copy).then_inc(S_att_rdy, 1)

            def result(b):
                act.wait_ge(S_b3, 1)
                act.wait_ge(S_out_dma, 16 * b)
                for c in range(NC_):
                    act.wait_ge(S_l3_ps, 2 * b + c + 1)
                    nc.scalar.activation(res[:, c], ps_q[:, c], ACT.Identity,
                                         bias=bias3[:, c, b:b + 1]).then_inc(S_res_rdy, 1)

            relu(0)
            demodulate(0)
            for n in range(4):
                act.wait_ge(S_urow_ps, n + 1)
                src = (ps_s, ps_s, ps_o, ps_o)[n][:, n % 2].rearrange("p m l -> p (m l)")
                nc.scalar.activation(urow[:, n].rearrange("p k i -> p (k i)"), src, ACT.Copy).then_inc(S_urow_sb, 1)

            def batch(b, nxt):
                if nxt:
                    relu(b + 1)
                exponentials(b, 0)
                if nxt:
                    demodulate(b + 1)
                exponentials(b, 1)
                attention_copy(b)
                result(b)

            for b in range(B):
                batch(b, b + 1 < B)

        @block.vector
        def _(dve):
            v = nc.vector
            v.memset(ps_s[:], 0.0)
            v.memset(ps_o[:], 0.0).then_inc(S_zeroed, 1)
            v.memset(cond_z[:], 0.0).then_inc(S_zeroed, 1)
            dve.wait_ge(S_par_in, 16)
            dve.wait_ge(S_zeroed, 2)
            v.tensor_copy(cond_b[:], cond.rearrange("p (b o) -> p b o", o=1).to_broadcast([P, B, P])).then_inc(S_conds, 1)
            v.tensor_copy(cond_z[:, 0:B], cond).then_inc(S_conds, 1)
            dve.wait_ge(S_style_ps, 1)
            for l in range(MOD):
                for c in range(NC_):
                    n = l * NC_ + c
                    v.tensor_scalar(style[:, l, c], ps_p[:, 0, B * n:B * n + B], GAIN if l == 0 else 1.0,
                                    affb[:, n:n + 1], ALU.mult, ALU.add).then_inc(S_styled, 1)
            dve.wait_ge(S_styled, 6)
            v.tensor_tensor(style_sq[:], style[:], style[:], ALU.mult).then_inc(S_style_sqs, 1)
            dve.wait_ge(S_style_sqs, 1)
            v.tensor_copy(ksq_b[:], style_sq[:, 1].rearrange("p c (b o) -> p c b o", o=1).to_broadcast([P, NC_, B, P])).then_inc(S_style_sqs, 1)
            dve.wait_ge(S_gbd_ps, 1)
            v.tensor_copy(gb_down[:], ps_p[:, 1].rearrange("p (b g h) -> p b g h", b=B, g=2)).then_inc(S_gbd, 1)
            dve.wait_ge(S_var_ps, 1)
            v.tensor_scalar(var[:, 0:B * D], ps_o[:].rearrange("p b m l -> p (b m l)"), EPS, None, ALU.add).then_inc(S_vars, 1)
            v.tensor_scalar(var[:, B * D:], ps_p[:, 0, 64:64 + 2 * NC_ * B], EPS, None, ALU.add).then_inc(S_vars, 1)
            dve.wait_ge(S_roots, 1)
            v.reciprocal(dem[:], root[:]).then_inc(S_dems, 1)
            dve.wait_ge(S_dems, 1)
            v.tensor_tensor(root[:], dem[:], dem[:], ALU.mult).then_inc(S_dems, 1)
            dve.wait_ge(S_dems, 2)
            v.tensor_tensor(root[:], root[:], var[:], ALU.mult).then_inc(S_dems, 1)
            dve.wait_ge(S_dems, 3)
            v.tensor_scalar(root[:], root[:], -0.5, 1.5, ALU.mult, ALU.add).then_inc(S_dems, 1)
            dve.wait_ge(S_dems, 4)
            v.tensor_tensor(dem[:], dem[:], root[:], ALU.mult).then_inc(S_newton, 1)

            def layer0_residual(b):
                dve.wait_ge(S_x_in, 16 * b + 16)
                dve.wait_ge(S_l1_ps, 2 * b)
                for c in range(NC_):
                    dve.wait_ge(S_up_ps, 2 * b + c + 1)
                    v.scalar_tensor_tensor(x0[:, c], x_sb[:, b, c], 2.0, ps_p[:, c], ALU.mult, ALU.add).then_inc(S_x0_rdy, 1)

            def layer1_residual(b):
                dve.wait_ge(S_k_ps, 2 * b)
                dve.wait_ge(S_x1b_rdy, 2 * b)
                for c in range(NC_):
                    dve.wait_ge(S_y_rdy, 2 * b + c + 1)
                    v.tensor_scalar(y1[:, c], y1[:, c], -CLAMP, CLAMP, ALU.max, ALU.min).then_inc(S_clipped, 1)
                for c in range(NC_):
                    dve.wait_ge(S_clipped, 2 * b + c + 1)
                    v.tensor_tensor(x1[:, c], x0[:, c], y1[:, c], ALU.add).then_inc(S_x1_rdy, 1)

            def keys(b, t):
                n = 2 * b + t
                dve.wait_ge(S_k_ps, n + 1)
                dve.wait_ge(S_kb_in, 16)
                v.tensor_tensor(kx[t][:], ps_p[:, t].rearrange("p (u h d) -> p u h d", u=U, h=NH),
                                kb_b[:].rearrange("p (o h) d -> p o h d", o=1).to_broadcast([P, U, NH, HD]), ALU.add).then_inc(S_kx_rdy, 1)
                dve.wait_ge(S_kx_rdy, n + 1)
                dve.wait_ge(S_s_ps, 2 * b)
                v.transpose(kT[t][:], kx[t][:].rearrange("p u h d -> p h u d")).then_inc(S_kT_rdy, 1)
                dve.wait_ge(S_kT_rdy, n + 1)
                for u in range(U):
                    v.tensor_scalar(kTz[t][:, u], kT[t][:], half[u], None, ALU.mult).then_inc(S_kTz_rdy, 1)

            def values(b, t):
                n = 2 * b + t
                dve.wait_ge(S_o_ps, 2 * b)
                v.transpose(vT[t][:], kx[t][:].rearrange("p u j d -> p d u j")).then_inc(S_vT_rdy, 1)

            def softmax_shift(b, t):
                n = 2 * b + t
                dve.wait_ge(S_s_ps, n + 1)
                v.transpose(sc[:], ps_s[:].rearrange("p b m l -> p m b l")).then_inc(S_sc_rdy, 1)
                dve.wait_ge(S_sc_rdy, n + 1)
                v.reduce_max(mx[:], sc[:, :, 0:NH], AX.X).then_inc(S_mx_rdy, 1)
                dve.wait_ge(S_mx_rdy, n + 1)
                v.tensor_tensor(sh[:], sc[:, :, 0:NH],
                                mx[:].rearrange("p (m o) -> p m o", o=1).to_broadcast([P, U * NH, NH]),
                                ALU.subtract).then_inc(S_sh_rdy, 1)

            def softmax_norm(b, t):
                n = 2 * b + t
                dve.wait_ge(S_ex_rdy, n + 1)
                v.reduce_sum(zs[:], ex[:], AX.X).then_inc(S_zs_rdy, 1)
                dve.wait_ge(S_zs_rdy, n + 1)
                v.reciprocal(rz[:], zs[:]).then_inc(S_rz_rdy, 1)
                dve.wait_ge(S_rz_rdy, n + 1)
                v.tensor_tensor(pn[:], ex[:], rz[:].rearrange("p (m o) -> p m o", o=1).to_broadcast([P, U * NH, NH]),
                                ALU.mult).then_inc(S_pn_rdy, 1)
                dve.wait_ge(S_pn_rdy, n + 1)
                v.transpose(pT[:], pn[:].rearrange("p (u h) j -> p h u j", u=U)).then_inc(S_pT_rdy, 1)
                dve.wait_ge(S_pT_rdy, n + 1)
                dve.wait_ge(S_o_ps, 2 * b)
                for u in range(U):
                    v.tensor_scalar(pTz[t][:, u], pT[:], half[u], None, ALU.mult).then_inc(S_pTz_rdy, 1)

            def attention_out(b, t):
                n = 2 * b + t
                dve.wait_ge(S_o_ps, n + 1)
                dve.wait_ge(S_tr_ps, 2 * b)
                v.transpose(ot[t][:].rearrange("p u d h -> p u h d"),
                            ps_o[:].rearrange("p b m l -> p m b l")).then_inc(S_ot_rdy, 1)

            def layer3_weight(b):
                dve.wait_ge(S_l3_ps, 2 * b)
                dve.wait_ge(S_w3_ps, b + 1)
                for c in range(NC_):
                    eye = con[:, P * (1 - c):P * (1 - c) + D]
                    v.tensor_tensor(w_3[:, c], ps_q[:, 1, D * c:D * c + D], eye, ALU.add).then_inc(S_w3_rdy, 1)

            def layer2_residual(b):
                dve.wait_ge(S_x1b_rdy, 2 * b + 2)
                dve.wait_ge(S_l3_ps, 2 * b)
                for c in range(NC_):
                    dve.wait_ge(S_op_ps, 2 * b + c + 1)
                    v.scalar_tensor_tensor(x2[:, c], ps_p[:, c], dem_1o[:, 1, c, b:b + 1], x1b[:, c],
                                           ALU.mult, ALU.add).then_inc(S_x2_rdy, 1)

            dve.wait_ge(S_con_in, 16)
            layer0_residual(0)
            layer1_residual(0)
            keys(0, 0)
            keys(0, 1)
            dve.wait_ge(S_ub_ps, 1)
            v.tensor_scalar(ub_sb[:], ps_q[0:RANK, 0, 0:B], bdec_sb[:, D:D + 1], None, ALU.add).then_inc(S_ub_added, 1)
            dve.wait_ge(S_b3_ps, 1)
            v.tensor_copy(bias3[:], ps_q[:, 0, 64:64 + NC_ * B].rearrange("p (c b) -> p c b", c=NC_)).then_inc(S_b3, 1)

            def batch(b, nxt):
                values(b, 0)
                values(b, 1)
                softmax_shift(b, 0)
                layer3_weight(b)
                softmax_norm(b, 0)
                if nxt:
                    layer0_residual(b + 1)
                softmax_shift(b, 1)
                softmax_norm(b, 1)
                if nxt:
                    layer1_residual(b + 1)
                attention_out(b, 0)
                if nxt:
                    keys(b + 1, 0)
                attention_out(b, 1)
                if nxt:
                    keys(b + 1, 1)
                layer2_residual(b)

            for b in range(B):
                batch(b, b + 1 < B)

        @block.tensor
        def _(pe):
            mm = nc.tensor.matmul

            pe.wait_ge(S_par_in, 16)
            for l in range(MOD):
                for c in range(NC_):
                    n = l * NC_ + c
                    last = mm(ps_p[:, 0, B * n:B * n + B], aff[:, l, P * c:P * c + P], cond, start=True, stop=True)
            last.then_inc(S_style_ps, 1)
            pe.wait_ge(S_conds, 1)
            for b in range(B):
                last = mm(ps_p[:, 1, P * b:P * b + P], cond_b[:, b], gbd_raw, start=True, stop=True)
            last.then_inc(S_gbd_ps, 1)
            for b in range(B):
                if b >= 2:
                    pe.wait_ge(S_gbu, b - 1)
                mm(ps_q[0:HID, b % 2], cond_b[:, b, 0:HID], gbu_raw, start=True, stop=True).then_inc(S_gbu_ps, 1)
            pe.wait_ge(S_squares, 1)
            pe.wait_ge(S_style_sqs, 2)
            pe.wait_ge(S_zeroed, 1)
            for b in range(B):
                for c in range(NC_):
                    mm(ps_o[:].rearrange("p b m l -> p (b m l)")[:, D * b:D * b + D], ksq_b[:, c, b], w_sq[:, 1, c],
                       start=c == 0, stop=c == NC_ - 1)
            for i, l in enumerate((0, 2)):
                for h in range(NC_):
                    for c in range(NC_):
                        at = 64 + B * (NC_ * i + h)
                        last = mm(ps_p[:, 0, at:at + B], w_sq[:, l, c, P * h:P * h + P], style_sq[:, l, c],
                                  start=c == 0, stop=c == NC_ - 1)
            last.then_inc(S_var_ps, 1)

            def down(b, first=False):
                pe.wait_ge(S_x_in, 16 * b + 16)
                pe.wait_ge(S_wdown_rdy, b + 1)
                if first:
                    pe.wait_ge(S_gbu, B)
                else:
                    pe.wait_ge(S_res_rdy, 2 * (b - 1))
                for c in range(NC_):
                    last = mm(ps_q[0:HID, 0], w_down[:, c], x_sb[:, b, c], start=c == 0, stop=c == NC_ - 1)
                last.then_inc(S_down_ps, 1)

            def layer3_weight(b):
                pe.wait_ge(S_u_added, 1)
                pe.wait_ge(S_res_rdy, 2 * b)
                for c in range(NC_):
                    last = mm(ps_q[:, 1, D * c:D * c + D], u_sb[:, b, P * c:P * c + P], v_sb[:], start=True, stop=True)
                last.then_inc(S_w3_ps, 1)

            def up(b, first=False):
                pe.wait_ge(S_hid_rdy, b + 1)
                pe.wait_ge(S_wup_rdy, b + 1)
                if first:
                    pe.wait_ge(S_vars, 2)
                else:
                    pe.wait_ge(S_x2_rdy, 2 * (b - 1))
                for c in range(NC_):
                    mm(ps_p[:, c], w_up[:, P * c:P * c + P], hid[:], start=True, stop=True).then_inc(S_up_ps, 1)

            def layer1(b):
                pe.wait_ge(S_wl1_rdy, 2 * b + 2)
                pe.wait_ge(S_x0_rdy, 2 * b + 2)
                pe.wait_ge(S_w3_rdy, 2 * b)
                for h in range(NC_):
                    for c in range(NC_):
                        last = mm(ps_q[:, h], w_l1[:, c, P * h:P * h + P], x0[:, c], start=c == 0, stop=c == NC_ - 1)
                    last.then_inc(S_l1_ps, 1)

            def keys(b, t):
                pe.wait_ge(S_wk_rdy, 2 * b + 2)
                pe.wait_ge(S_x1_rdy, 2 * b + 2)
                for u in range(U):
                    for c in range(NC_):
                        at = TOK * t + P * u
                        last = mm(ps_p[:, t, D * u:D * u + D], x1[:, c, at:at + P], w_k[:, c],
                                  start=c == 0, stop=c == NC_ - 1)
                last.then_inc(S_k_ps, 1)

            def scores(b, t):
                n = 2 * b + t
                pe.wait_ge(S_kTz_rdy, 2 * n + 2)
                pe.wait_ge(S_sc_rdy, n)
                for p in range(STRIP):
                    for g in range(G):
                        r = slice(STRIP * g, STRIP * g + STRIP)
                        last = mm(ps_s[STRIP * g:STRIP * g + NH, p // PL, :, p % PL], kT[t][r, :, p],
                                  kTz[t][r, :, :, p], start=True, stop=True)
                last.then_inc(S_s_ps, 1)

            def attend(b, t):
                n = 2 * b + t
                pe.wait_ge(S_pTz_rdy, 2 * n + 2)
                pe.wait_ge(S_vT_rdy, n + 1)
                pe.wait_ge(S_ot_rdy, n)
                for p in range(STRIP):
                    for g in range(G):
                        r = slice(STRIP * g, STRIP * g + STRIP)
                        last = mm(ps_o[STRIP * g:STRIP * g + HD, p // PL, :, p % PL], vT[t][r, :, p],
                                  pTz[t][r, :, :, p], start=True, stop=True)
                last.then_inc(S_o_ps, 1)

            def transposes(b, nxt):
                pe.wait_ge(S_ot_rdy, 2 * b + 2)
                if nxt:
                    pe.wait_ge(S_y_rdy, 2 * b + 4)
                else:
                    pe.wait_ge(S_w3_rdy, 2 * b + 2)
                for h in range(NC_):
                    for t in range(TILES):
                        for u in range(U):
                            at = TOK * t + P * u
                            d = HD // NC_ * h
                            last = nc.tensor.transpose(ps_q[:, h, at:at + P], ot[t][:, u, d:d + HD // NC_].rearrange("p d h -> p (d h)"), ident)
                    last.then_inc(S_tr_ps, 1)

            def layer2_out(b, nxt):
                pe.wait_ge(S_wo_rdy, 2 * b + 2)
                pe.wait_ge(S_att_rdy, 2 * b + 2)
                if nxt:
                    pe.wait_ge(S_kx_rdy, 2 * b + 4)
                for h in range(NC_):
                    for c in range(NC_):
                        last = mm(ps_p[:, h], w_o[:, c, P * h:P * h + P], att[:, c], start=c == 0, stop=c == NC_ - 1)
                    last.then_inc(S_op_ps, 1)

            def layer3(b):
                pe.wait_ge(S_w3_rdy, 2 * b + 2)
                pe.wait_ge(S_x2_rdy, 2 * b + 2)
                for h in range(NC_):
                    for c in range(NC_):
                        last = mm(ps_q[:, h], w_3[:, c, P * h:P * h + P], x2[:, c], start=c == 0, stop=c == NC_ - 1)
                    last.then_inc(S_l3_ps, 1)

            down(0, first=True)
            up(0, first=True)
            layer1(0)
            keys(0, 0)
            keys(0, 1)
            pe.wait_ge(S_dec_in, 64)
            pe.wait_ge(S_conds, 2)
            pe.wait_ge(S_vars, 1)
            for n in range(4):
                for g in range(G):
                    j = G * n + g
                    bank = (ps_s, ps_s, ps_o, ps_o)[n][STRIP * g:STRIP * g + STRIP, n % 2].rearrange("p m l -> p (m l)")
                    if j < NCH:
                        last = mm(bank, cond_z[:], wdec_sb[:, 2 * j:2 * j + 2], start=True, stop=True)
                last.then_inc(S_urow_ps, 1)
            pe.wait_ge(S_y_rdy, 2)
            mm(ps_q[0:RANK, 0, 0:B], wdecb_sb[:], cond, start=True, stop=True).then_inc(S_ub_ps, 1)
            pe.wait_ge(S_ub_added, 1)
            for h in range(NC_):
                last = mm(ps_q[:, 0, 64 + B * h:64 + B * h + B], v_sb[:, P * h:P * h + P], ub_sb[:], start=True, stop=True)
            last.then_inc(S_b3_ps, 1)
            pe.wait_ge(S_urow_sb, 4)
            pe.wait_ge(S_b3, 1)

            def batch(b, nxt):
                scores(b, 0)
                if nxt:
                    down(b + 1)
                layer3_weight(b)
                if nxt:
                    up(b + 1)
                scores(b, 1)
                if nxt:
                    layer1(b + 1)
                attend(b, 0)
                if nxt:
                    keys(b + 1, 0)
                attend(b, 1)
                if nxt:
                    keys(b + 1, 1)
                transposes(b, nxt)
                layer2_out(b, nxt)
                layer3(b)

            for b in range(B):
                batch(b, b + 1 < B)


def kernel(x, cond_512, L0_cond_down_project, L0_cond_down_gamma, L0_cond_down_beta,
           L0_cond_up_project, L0_cond_up_gamma, L0_cond_up_beta, L1_cond_weight, L1_cond_bias,
           L1_cond_affine_w, L1_cond_affine_b, L2_cond_k_aff_w, L2_cond_k_aff_b, L2_cond_k_w,
           L2_cond_k_b, L2_cond_o_aff_w, L2_cond_o_aff_b, L2_cond_o_w, L2_cond_o_b, L3_cond_W_dec,
           L3_cond_b_dec, L3_cond_V):
    import concourse.bacc as bacc
    from concourse.bass_utils import run_bass_kernel_spmd

    def halves(a):
        a = np.asarray(a).reshape(NC_, P, -1)
        return a.transpose(1, 0, 2).reshape(P, -1)

    def by_dim(a):
        a = np.asarray(a)
        return a.reshape((NH, HD) + a.shape[1:]).swapaxes(0, 1).reshape(a.shape)

    up = np.zeros((P, D), np.float32)
    up[:HID] = np.asarray(L0_cond_up_project)
    params = np.concatenate(
        [np.asarray(cond_512).T]
        + [halves(a) for a in (L1_cond_affine_b, L2_cond_k_aff_b, by_dim(L2_cond_o_aff_b), L1_cond_bias, L2_cond_o_b)]
        + [np.asarray(a).T for a in (L1_cond_affine_w, L2_cond_k_aff_w, by_dim(L2_cond_o_aff_w))]
        + [halves(L0_cond_down_project)]
        + [np.asarray(a) for a in (L0_cond_down_gamma, L0_cond_down_beta, L0_cond_up_gamma, L0_cond_up_beta)]
        + [up], axis=1)
    weights = np.stack([halves(np.asarray(a).T) for a in (L1_cond_weight, L2_cond_k_w)]
                       + [halves(by_dim(np.asarray(L2_cond_o_w).T))], axis=1)
    wdec = np.asarray(L3_cond_W_dec).reshape(C, D + 1, RANK).transpose(0, 2, 1)
    eye = np.zeros((P, CONSTW), np.float32)
    eye[:, P:2 * P] = np.eye(P)
    for u in range(U):
        eye[:, 3 * P + u] = np.arange(P) % STRIP // (STRIP // U) == u
    arrays = {
        "xT": np.asarray(x).reshape(B, S, NC_, P).transpose(3, 0, 2, 1),
        "params": params,
        "weights": weights.reshape(P, MOD, NC_, D),
        "kb": np.asarray(L2_cond_k_b).reshape(1, D),
        "wdec": wdec[:, :, :D],
        "wdecb": wdec[:, :, D],
        "bdec": np.asarray(L3_cond_b_dec).reshape(D + 1, RANK).T,
        "vmat": np.asarray(L3_cond_V),
        "consts": eye,
    }
    arrays = {k: np.ascontiguousarray(a) for k, a in arrays.items()}
    nc = bacc.Bacc("TRN2", target_bir_lowering=False, num_devices=1)
    args = [nc.dram_tensor(k, a.shape, mybir.dt.from_np(a.dtype), kind="ExternalInput").ap() for k, a in arrays.items()]
    out = nc.dram_tensor("outT", (P, B, NC_, S), mybir.dt.float32, kind="ExternalOutput").ap()
    cond_resid_kernel(nc, *args, out)
    r = run_bass_kernel_spmd(nc, [arrays], core_ids=[0])
    got = r.results[0]["outT"]
    return np.ascontiguousarray(got.transpose(1, 3, 2, 0).reshape(B, S, D))
```

```python
import numpy as np

import concourse.bass as bass
from concourse import mybir

B, S, D, C = 4, 512, 256, 128
HID = 64
NH, HD = 16, 16
RANK = 30
P = 128
NC_ = D // P
TILES = 2
TOK = S // TILES
U = 2
STRIP = 32
G = P // STRIP
PL = STRIP // 2
MOD = 3
CHUNK = 2 * D
NCH = RANK // 2
GAIN = float(1.0 / np.sqrt(C).astype(np.float32))
EPS = 1e-8
CLAMP = 256.0

PAR = {}
_at = 0
for _n, _w in (("cond", B), ("affb", MOD * NC_), ("outb", 2 * NC_), ("aff", MOD * D),
               ("down", NC_ * HID), ("gbdown", 2 * HID), ("gbup", 2 * D), ("up", D)):
    PAR[_n] = slice(_at, _at + _w)
    _at += _w
PARW = _at
CONSTW = 3 * P + U + B * P


def cond_resid_kernel(nc, xT, params, weights, kb, wdec, wdecb, bdec, vmat, consts, outT):
    f32 = mybir.dt.float32
    ALU = mybir.AluOpType
    ACT = mybir.ActivationFunctionType
    AX = mybir.AxisListType
    from contextlib import ExitStack

    ctx = ExitStack()
    with ctx:
        def sb(name, shape):
            return ctx.enter_context(nc.sbuf_tensor(name, shape, f32))

        def sem(name):
            return ctx.enter_context(nc.semaphore(name))

        par = sb("par", [P, PARW])
        w_raw = sb("w_raw", [P, MOD, NC_, D])
        w_sq = sb("w_sq", [P, MOD, NC_, D])
        kb_b = sb("kb_b", [P, NH, HD])
        wdec_sb = sb("wdec_sb", [P, RANK, D])
        wdecb_sb = sb("wdecb_sb", [P, RANK])
        bdec_sb = sb("bdec_sb", [RANK, D + 1])
        v_sb = sb("v_sb", [RANK, D])
        con = sb("con", [P, CONSTW])
        x_sb = sb("x_sb", [P, B, NC_, S])
        cond_b = sb("cond_b", [P, B, P])
        cond_z = sb("cond_z", [P, STRIP])
        style = sb("style", [P, MOD, NC_, B])
        style_sq = sb("style_sq", [P, MOD, NC_, B])
        var_k = sb("var_k", [B, D])
        root_k = sb("root_k", [B, D])
        rec_k = sb("rec_k", [B, D])
        corr_k = sb("corr_k", [B, D])
        norm_k = sb("norm_k", [B, D])
        dem_k = sb("dem_k", [P, B, D])
        var_o = sb("var_o", [P, 2, NC_, B])
        root_o = sb("root_o", [P, 2, NC_, B])
        rec_o = sb("rec_o", [P, 2, NC_, B])
        corr_o = sb("corr_o", [P, 2, NC_, B])
        dem_o = sb("dem_o", [P, 2, NC_, B])
        gb_down = sb("gb_down", [P, B, 2, HID])
        gb_up = sb("gb_up", [HID, B, 2, D])
        urow = sb("urow", [P, 4, 2, D])
        u_sb = sb("u_sb", [RANK, B, D])
        ub_sb = sb("ub_sb", [RANK, B])
        bias3 = sb("bias3", [P, NC_, B])
        w_down = sb("w_down", [P, NC_, HID])
        w_up = sb("w_up", [HID, D])
        w_l1 = sb("w_l1", [P, NC_, D])
        w_k = sb("w_k", [P, NC_, D])
        w_o = sb("w_o", [P, NC_, D])
        w_3 = sb("w_3", [P, NC_, D])
        hid = sb("hid", [HID, S])
        x0 = sb("x0", [P, NC_, S])
        y1 = sb("y1", [P, NC_, S])
        x1 = sb("x1", [P, NC_, S])
        x1b = sb("x1b", [P, NC_, S])
        x2 = sb("x2", [P, NC_, S])
        att = sb("att", [P, NC_, S])
        res = sb("res", [P, NC_, S])
        kx = [sb(f"kx{t}", [P, U, NH, HD]) for t in range(TILES)]
        kT = [sb(f"kT{t}", [P, NH, STRIP]) for t in range(TILES)]
        kTz = [sb(f"kTz{t}", [P, U, NH, STRIP]) for t in range(TILES)]
        vT = [sb(f"vT{t}", [P, HD, STRIP]) for t in range(TILES)]
        sc = sb("sc", [P, U * NH, STRIP])
        mx = sb("mx", [P, U * NH])
        sh = sb("sh", [P, U * NH, NH])
        ex = sb("ex", [P, U * NH, NH])
        zs = sb("zs", [P, U * NH])
        rz = sb("rz", [P, U * NH])
        pn = sb("pn", [P, U * NH, NH])
        pT = sb("pT", [P, NH, STRIP])
        pTz = [sb(f"pTz{t}", [P, U, NH, STRIP]) for t in range(TILES)]
        ot = [sb(f"ot{t}", [P, U, STRIP, NH]) for t in range(TILES)]

        urow_d = nc.dram_tensor("urow_d", [B, 4, G, 2, D], f32, kind="Internal").ap()

        ps_a = [ctx.enter_context(nc.psum_tensor(f"ps_a{i}", [P, 2, U * NH, PL], f32)) for i in range(2)]
        ps_p = ctx.enter_context(nc.psum_tensor("ps_p", [P, 2, S], f32))
        ps_q = ctx.enter_context(nc.psum_tensor("ps_q", [P, 2, S], f32))

        pick = [con[0:B, 3 * P + U + P * b:3 * P + U + P * b + P] for b in range(B)]
        flat_a = [a[:].rearrange("p b m l -> p b (m l)") for a in ps_a]
        ident = con[:, P:2 * P]
        half = [con[:, 3 * P + u:3 * P + u + 1] for u in range(U)]
        cond = par[:, PAR["cond"]]
        affb = par[:, PAR["affb"]]
        outb = par[:, PAR["outb"]]
        aff = par[:, PAR["aff"]].rearrange("p (l i) -> p l i", l=MOD)
        wd_raw = par[:, PAR["down"]].rearrange("p (c h) -> p c h", c=NC_)
        gbd_raw = par[:, PAR["gbdown"]]
        gbu_raw = par[:, PAR["gbup"]]
        wu_raw = par[0:HID, PAR["up"]]

        S_par_in = sem("par_in")
        S_w_in = sem("w_in")
        S_kb_in = sem("kb_in")
        S_con_in = sem("con_in")
        S_dec_in = sem("dec_in")
        S_x_in = sem("x_in")
        S_out_dma = sem("out_dma")
        S_ur_out = sem("ur_out")
        S_ur_in = sem("ur_in")
        S_zeroed = sem("zeroed")
        S_cond_rep = sem("cond_rep")
        S_cond_pad = sem("cond_pad")
        S_style_ps = sem("style_ps")
        S_styled = sem("styled")
        S_squares = sem("squares")
        S_style_sq = sem("style_sq")
        S_varo_ps = sem("varo_ps")
        S_vark_ps = sem("vark_ps")
        S_varo_in = sem("varo_in")
        S_vark_in = sem("vark_in")
        S_rooto_rdy = sem("rooto_rdy")
        S_rootk_rdy = sem("rootk_rdy")
        S_demo_step = sem("demo_step")
        S_demk_step = sem("demk_step")
        S_demo_rdy = sem("demo_rdy")
        S_normk_rdy = sem("normk_rdy")
        S_demk_ps = sem("demk_ps")
        S_demk_rdy = sem("demk_rdy")
        S_gbd_ps = sem("gbd_ps")
        S_gbd_rdy = sem("gbd_rdy")
        S_gbu_ps = sem("gbu_ps")
        S_gbu_rdy = sem("gbu_rdy")
        S_urow_ps = sem("urow_ps")
        S_urow_rdy = sem("urow_rdy")
        S_u_added = sem("u_added")
        S_ub_added = sem("ub_added")
        S_ub_ps = sem("ub_ps")
        S_b3_ps = sem("b3_ps")
        S_b3_rdy = sem("b3_rdy")
        S_wdown_scaled = sem("wdown_scaled")
        S_wup_scaled = sem("wup_scaled")
        S_wk_scaled = sem("wk_scaled")
        S_wdown_rdy = sem("wdown_rdy")
        S_wup_rdy = sem("wup_rdy")
        S_wl1_rdy = sem("wl1_rdy")
        S_wk_rdy = sem("wk_rdy")
        S_wo_rdy = sem("wo_rdy")
        S_w3_ps = sem("w3_ps")
        S_w3_rdy = sem("w3_rdy")
        S_down_ps = sem("down_ps")
        S_hid_rdy = sem("hid_rdy")
        S_up_ps = sem("up_ps")
        S_x0_rdy = sem("x0_rdy")
        S_l1_ps = sem("l1_ps")
        S_y_rdy = sem("y_rdy")
        S_clipped = sem("clipped")
        S_x1_rdy = sem("x1_rdy")
        S_x1b_rdy = sem("x1b_rdy")
        S_k_ps = sem("k_ps")
        S_kx_rdy = sem("kx_rdy")
        S_kT_rdy = sem("kT_rdy")
        S_kTz_rdy = sem("kTz_rdy")
        S_vT_rdy = sem("vT_rdy")
        S_s_ps = sem("s_ps")
        S_sc_rdy = sem("sc_rdy")
        S_mx_rdy = sem("mx_rdy")
        S_sh_rdy = sem("sh_rdy")
        S_ex_rdy = sem("ex_rdy")
        S_zs_rdy = sem("zs_rdy")
        S_rz_rdy = sem("rz_rdy")
        S_pn_rdy = sem("pn_rdy")
        S_pT_rdy = sem("pT_rdy")
        S_pTz_rdy = sem("pTz_rdy")
        S_o_ps = sem("o_ps")
        S_ot_rdy = sem("ot_rdy")
        S_tr_ps = sem("tr_ps")
        S_att_rdy = sem("att_rdy")
        S_op_ps = sem("op_ps")
        S_x2_rdy = sem("x2_rdy")
        S_l3_ps = sem("l3_ps")
        S_res_rdy = sem("res_rdy")

        block = ctx.enter_context(nc.Block())

        @block.sync
        def _(sp):
            sp.dma_start(par[:], params).then_inc(S_par_in, 16)
            sp.dma_start(x_sb[:, 0], xT[:, 0]).then_inc(S_x_in, 16)
            sp.dma_start(wdec_sb[:], wdec).then_inc(S_dec_in, 16)
            sp.dma_start(wdecb_sb[:], wdecb).then_inc(S_dec_in, 16)
            sp.dma_start(bdec_sb[:], bdec).then_inc(S_dec_in, 16)
            sp.dma_start(v_sb[:], vmat).then_inc(S_dec_in, 16)
            for b in range(1, B):
                sp.wait_ge(S_x_in, 16 * b)
                sp.dma_start(x_sb[:, b], xT[:, b]).then_inc(S_x_in, 16)
            sp.wait_ge(S_urow_rdy, 4)
            for g in range(G):
                slots = 4 if 3 * G + g < NCH else 3
                sp.dma_start(urow_d[:, 0:slots, g], urow[STRIP * g:STRIP * g + B, 0:slots]).then_inc(S_ur_out, 16)
            sp.wait_ge(S_ur_out, 16 * G)
            sp.dma_start(u_sb[:], urow_d.rearrange("b n g k i -> (n g k) b i")[0:RANK]).then_inc(S_ur_in, 16)

            for b in range(B):
                sp.wait_ge(S_res_rdy, 2 * b + 2)
                sp.dma_start(outT[:, b], res[:]).then_inc(S_out_dma, 16)
            sp.wait_ge(S_out_dma, 16 * B)

        @block.gpsimd
        def _(pool):
            def weights_down_up(b):
                pool.wait_ge(S_gbd_rdy, b + 1)
                pool.wait_ge(S_down_ps, b)
                gd = gb_down[:, b, 0:1].to_broadcast([P, NC_, HID])
                bd = gb_down[:, b, 1:2].to_broadcast([P, NC_, HID])
                pool.tensor_tensor(w_down[:], wd_raw, gd, ALU.mult).then_inc(S_wdown_scaled, 1)
                pool.wait_ge(S_wdown_scaled, b + 1)
                pool.tensor_tensor(w_down[:], w_down[:], bd, ALU.add).then_inc(S_wdown_rdy, 1)
                pool.wait_ge(S_gbu_rdy, b + 1)
                pool.wait_ge(S_up_ps, 2 * b)
                pool.tensor_tensor(w_up[:], wu_raw, gb_up[:, b, 0], ALU.mult).then_inc(S_wup_scaled, 1)
                pool.wait_ge(S_wup_scaled, b + 1)
                pool.tensor_tensor(w_up[:], w_up[:], gb_up[:, b, 1], ALU.add).then_inc(S_wup_rdy, 1)

            def weights_l1_k(b):
                pool.wait_ge(S_styled, 6)
                pool.wait_ge(S_l1_ps, 2 * b)
                for c in range(NC_):
                    pool.tensor_scalar(w_l1[:, c], w_raw[:, 0, c], style[:, 0, c, b:b + 1], 1.0,
                                       ALU.mult, ALU.mult).then_inc(S_wl1_rdy, 1)
                pool.wait_ge(S_k_ps, 2 * b)
                pool.wait_ge(S_demk_rdy, b + 1)
                for c in range(NC_):
                    pool.tensor_scalar(w_k[:, c], w_raw[:, 1, c], style[:, 1, c, b:b + 1], 1.0,
                                       ALU.mult, ALU.mult).then_inc(S_wk_scaled, 1)
                for c in range(NC_):
                    pool.wait_ge(S_wk_scaled, 2 * b + c + 1)
                    pool.tensor_tensor(w_k[:, c], w_k[:, c], dem_k[:, b], ALU.mult).then_inc(S_wk_rdy, 1)

            def weights_o(b):
                pool.wait_ge(S_op_ps, 2 * b)
                for c in range(NC_):
                    pool.tensor_scalar(w_o[:, c], w_raw[:, 2, c], style[:, 2, c, b:b + 1], 1.0,
                                       ALU.mult, ALU.mult).then_inc(S_wo_rdy, 1)

            def residual_bias(b):
                pool.wait_ge(S_x1_rdy, 2 * b + 2)
                pool.wait_ge(S_x2_rdy, 2 * b)
                for c in range(NC_):
                    pool.tensor_scalar(x1b[:, c], x1[:, c], 1.0, outb[:, NC_ + c:NC_ + c + 1],
                                       ALU.mult, ALU.add).then_inc(S_x1b_rdy, 1)

            pool.wait_ge(S_par_in, 16)
            pool.wait_ge(S_w_in, 16)
            weights_down_up(0)
            weights_l1_k(0)
            pool.wait_ge(S_dec_in, 64)
            residual_bias(0)
            pool.wait_ge(S_ur_in, 16)
            pool.tensor_tensor(u_sb[:], u_sb[:], bdec_sb[:, 0:D].rearrange("k (o i) -> k o i", o=1).to_broadcast([RANK, B, D]),
                               ALU.add).then_inc(S_u_added, 1)

            def batch(b, nxt):
                if nxt:
                    weights_down_up(b + 1)
                    weights_l1_k(b + 1)
                weights_o(b)
                if nxt:
                    residual_bias(b + 1)

            for b in range(B):
                batch(b, b + 1 < B)

        @block.scalar
        def _(act):
            act.dma_start(con[:], consts).then_inc(S_con_in, 16)
            act.dma_start(w_raw[:], weights).then_inc(S_w_in, 16)
            act.dma_start(kb_b[:], kb.to_broadcast([P, D]).rearrange("p (h d) -> p h d", h=NH)).then_inc(S_kb_in, 16)
            act.wait_ge(S_w_in, 16)
            nc.scalar.activation(w_sq[:], w_raw[:], ACT.Square).then_inc(S_squares, 1)
            act.wait_ge(S_varo_in, 1)
            nc.scalar.activation(root_o[:], var_o[:], ACT.Sqrt).then_inc(S_rooto_rdy, 1)
            act.wait_ge(S_vark_in, 1)
            nc.scalar.activation(root_k[:], var_k[:], ACT.Sqrt).then_inc(S_rootk_rdy, 1)

            def gammas_up(b):
                act.wait_ge(S_gbu_ps, b + 1)
                nc.scalar.activation(gb_up[:, b].rearrange("h g i -> h (g i)"), flat_a[b % 2][0:HID, b // 2],
                                     ACT.Copy).then_inc(S_gbu_rdy, 1)

            def relu(b):
                act.wait_ge(S_down_ps, b + 1)
                act.wait_ge(S_up_ps, 2 * b)
                nc.scalar.activation(hid[:], ps_p[0:HID, 0], ACT.Relu).then_inc(S_hid_rdy, 1)

            def demodulate(b):
                act.wait_ge(S_demo_rdy, 1)
                for c in range(NC_):
                    act.wait_ge(S_l1_ps, 2 * b + c + 1)
                    act.wait_ge(S_x1_rdy, 2 * b)
                    nc.scalar.activation(y1[:, c], ps_q[:, c], ACT.Identity, bias=outb[:, c:c + 1],
                                         scale=dem_o[:, 0, c, b:b + 1]).then_inc(S_y_rdy, 1)

            def exponentials(b, t):
                act.wait_ge(S_sh_rdy, 2 * b + t + 1)
                act.wait_ge(S_pn_rdy, 2 * b + t)
                nc.scalar.activation(ex[:], sh[:], ACT.Exp, scale=HD ** -0.5).then_inc(S_ex_rdy, 1)

            def attention_copy(b):
                act.wait_ge(S_op_ps, 2 * b)
                for c in range(NC_):
                    act.wait_ge(S_tr_ps, 2 * b + c + 1)
                    nc.scalar.activation(att[:, c], ps_q[:, c], ACT.Copy).then_inc(S_att_rdy, 1)

            def result(b, c):
                act.wait_ge(S_b3_rdy, 1)
                act.wait_ge(S_out_dma, 16 * b)
                act.wait_ge(S_l3_ps, 2 * b + c + 1)
                nc.scalar.activation(res[:, c], ps_q[:, c], ACT.Identity,
                                     bias=bias3[:, c, b:b + 1]).then_inc(S_res_rdy, 1)

            gammas_up(0)
            relu(0)
            demodulate(0)
            for n in range(4):
                act.wait_ge(S_urow_ps, n + 1)
                nc.scalar.activation(urow[:, n].rearrange("p k i -> p (k i)"), flat_a[n % 2][:, n // 2],
                                     ACT.Copy).then_inc(S_urow_rdy, 1)
            for b in range(1, B):
                gammas_up(b)

            for b in range(B):
                nxt = b + 1 < B
                exponentials(b, 0)
                if nxt:
                    relu(b + 1)
                if b:
                    result(b - 1, 0)
                exponentials(b, 1)
                if b:
                    result(b - 1, 1)
                if nxt:
                    demodulate(b + 1)
                attention_copy(b)
            result(B - 1, 0)
            result(B - 1, 1)

        @block.vector
        def _(dve):
            v = nc.vector
            for a in ps_a:
                v.memset(a[:], 0.0).then_inc(S_zeroed, 1)
            v.memset(cond_z[:], 0.0).then_inc(S_zeroed, 1)
            dve.wait_ge(S_par_in, 16)
            v.tensor_copy(cond_b[:], cond.rearrange("p (b o) -> p b o", o=1).to_broadcast([P, B, P])).then_inc(S_cond_rep, 1)
            dve.wait_ge(S_style_ps, 1)
            for l in range(MOD):
                for c in range(NC_):
                    n = l * NC_ + c
                    v.tensor_scalar(style[:, l, c], ps_p[:, 1, B * n:B * n + B], GAIN if l == 0 else 1.0,
                                    affb[:, n:n + 1], ALU.mult, ALU.add).then_inc(S_styled, 1)
            dve.wait_ge(S_styled, 6)
            v.tensor_tensor(style_sq[:], style[:], style[:], ALU.mult).then_inc(S_style_sq, 1)

            def gammas_down(b):
                dve.wait_ge(S_gbd_ps, b + 1)
                v.tensor_copy(gb_down[:, b].rearrange("p g h -> p (g h)"), ps_q[:, 1, P * b:P * b + P]).then_inc(S_gbd_rdy, 1)

            gammas_down(0)
            dve.wait_ge(S_zeroed, 3)
            v.tensor_copy(cond_z[:, 0:B], cond).then_inc(S_cond_pad, 1)

            dve.wait_ge(S_varo_ps, 1)
            v.tensor_scalar(var_o[:].rearrange("p l c b -> p (l c b)"), ps_p[:, 1, 64:64 + 2 * NC_ * B], EPS, None,
                            ALU.add).then_inc(S_varo_in, 1)
            dve.wait_ge(S_vark_ps, 1)
            v.tensor_scalar(var_k[:], ps_q[0:B, 0, 0:D], EPS, None, ALU.add).then_inc(S_vark_in, 1)
            dve.wait_ge(S_rooto_rdy, 1)
            v.reciprocal(rec_o[:], root_o[:]).then_inc(S_demo_step, 1)
            dve.wait_ge(S_demo_step, 1)
            v.tensor_tensor(corr_o[:], rec_o[:], rec_o[:], ALU.mult).then_inc(S_demo_step, 1)
            dve.wait_ge(S_demo_step, 2)
            v.tensor_tensor(corr_o[:], corr_o[:], var_o[:], ALU.mult).then_inc(S_demo_step, 1)
            dve.wait_ge(S_demo_step, 3)
            v.tensor_scalar(corr_o[:], corr_o[:], -0.5, 1.5, ALU.mult, ALU.add).then_inc(S_demo_step, 1)
            dve.wait_ge(S_demo_step, 4)
            v.tensor_tensor(dem_o[:], rec_o[:], corr_o[:], ALU.mult).then_inc(S_demo_rdy, 1)
            dve.wait_ge(S_rootk_rdy, 1)
            v.reciprocal(rec_k[:], root_k[:]).then_inc(S_demk_step, 1)
            dve.wait_ge(S_demk_step, 1)
            v.tensor_tensor(corr_k[:], rec_k[:], rec_k[:], ALU.mult).then_inc(S_demk_step, 1)
            dve.wait_ge(S_demk_step, 2)
            v.tensor_tensor(corr_k[:], corr_k[:], var_k[:], ALU.mult).then_inc(S_demk_step, 1)
            dve.wait_ge(S_demk_step, 3)
            v.tensor_scalar(corr_k[:], corr_k[:], -0.5, 1.5, ALU.mult, ALU.add).then_inc(S_demk_step, 1)
            dve.wait_ge(S_demk_step, 4)
            v.tensor_tensor(norm_k[:], rec_k[:], corr_k[:], ALU.mult).then_inc(S_normk_rdy, 1)

            def demodulation_k(b):
                dve.wait_ge(S_demk_ps, b + 1)
                v.tensor_copy(dem_k[:, b], ps_q[:, b % 2, 0:D] if b == 0 else flat_a[0][:, 0, 0:D]).then_inc(S_demk_rdy, 1)

            def layer0_residual(b):
                dve.wait_ge(S_x_in, 16 * b + 16)
                dve.wait_ge(S_l1_ps, 2 * b)
                for c in range(NC_):
                    dve.wait_ge(S_up_ps, 2 * b + c + 1)
                    v.scalar_tensor_tensor(x0[:, c], x_sb[:, b, c], 2.0, ps_p[:, c], ALU.mult, ALU.add).then_inc(S_x0_rdy, 1)

            def layer1_residual(b):
                dve.wait_ge(S_k_ps, 2 * b)
                dve.wait_ge(S_x1b_rdy, 2 * b)
                for c in range(NC_):
                    dve.wait_ge(S_y_rdy, 2 * b + c + 1)
                    v.tensor_scalar(y1[:, c], y1[:, c], -CLAMP, CLAMP, ALU.max, ALU.min).then_inc(S_clipped, 1)
                for c in range(NC_):
                    dve.wait_ge(S_clipped, 2 * b + c + 1)
                    v.tensor_tensor(x1[:, c], x0[:, c], y1[:, c], ALU.add).then_inc(S_x1_rdy, 1)

            def keys(b, t):
                n = 2 * b + t
                dve.wait_ge(S_k_ps, n + 1)
                dve.wait_ge(S_kb_in, 16)
                v.tensor_tensor(kx[t][:], ps_p[:, t].rearrange("p (u h d) -> p u h d", u=U, h=NH),
                                kb_b[:].rearrange("p (o h) d -> p o h d", o=1).to_broadcast([P, U, NH, HD]), ALU.add).then_inc(S_kx_rdy, 1)
                dve.wait_ge(S_kx_rdy, n + 1)
                dve.wait_ge(S_s_ps, 2 * b)
                v.transpose(kT[t][:], kx[t][:].rearrange("p u h d -> p h u d")).then_inc(S_kT_rdy, 1)
                dve.wait_ge(S_kT_rdy, n + 1)
                for u in range(U):
                    v.tensor_scalar(kTz[t][:, u], kT[t][:], half[u], None, ALU.mult).then_inc(S_kTz_rdy, 1)

            def values(b, t):
                n = 2 * b + t
                dve.wait_ge(S_o_ps, 2 * b)
                v.transpose(vT[t][:], kx[t][:].rearrange("p u j d -> p d u j")).then_inc(S_vT_rdy, 1)

            def softmax_shift(b, t):
                n = 2 * b + t
                dve.wait_ge(S_s_ps, n + 1)
                v.transpose(sc[:], ps_a[t][:].rearrange("p b m l -> p m b l")).then_inc(S_sc_rdy, 1)
                dve.wait_ge(S_sc_rdy, n + 1)
                v.reduce_max(mx[:], sc[:, :, 0:NH], AX.X).then_inc(S_mx_rdy, 1)
                dve.wait_ge(S_mx_rdy, n + 1)
                v.tensor_tensor(sh[:], sc[:, :, 0:NH],
                                mx[:].rearrange("p (m o) -> p m o", o=1).to_broadcast([P, U * NH, NH]),
                                ALU.subtract).then_inc(S_sh_rdy, 1)

            def softmax_norm(b, t):
                n = 2 * b + t
                dve.wait_ge(S_ex_rdy, n + 1)
                v.reduce_sum(zs[:], ex[:], AX.X).then_inc(S_zs_rdy, 1)
                dve.wait_ge(S_zs_rdy, n + 1)
                v.reciprocal(rz[:], zs[:]).then_inc(S_rz_rdy, 1)
                dve.wait_ge(S_rz_rdy, n + 1)
                v.tensor_tensor(pn[:], ex[:], rz[:].rearrange("p (m o) -> p m o", o=1).to_broadcast([P, U * NH, NH]),
                                ALU.mult).then_inc(S_pn_rdy, 1)
                dve.wait_ge(S_pn_rdy, n + 1)
                v.transpose(pT[:], pn[:].rearrange("p (u h) j -> p h u j", u=U)).then_inc(S_pT_rdy, 1)
                dve.wait_ge(S_pT_rdy, n + 1)
                dve.wait_ge(S_o_ps, 2 * b)
                for u in range(U):
                    v.tensor_scalar(pTz[t][:, u], pT[:], half[u], None, ALU.mult).then_inc(S_pTz_rdy, 1)

            def attention_out(b, t):
                n = 2 * b + t
                dve.wait_ge(S_o_ps, n + 1)
                dve.wait_ge(S_tr_ps, 2 * b)
                v.transpose(ot[t][:].rearrange("p u d h -> p u h d"),
                            ps_a[1 - t][:].rearrange("p b m l -> p m b l")).then_inc(S_ot_rdy, 1)

            def layer3_weight(b):
                dve.wait_ge(S_l3_ps, 2 * b)
                dve.wait_ge(S_w3_ps, b + 1)
                for c in range(NC_):
                    eye = con[:, P * (1 - c):P * (1 - c) + D]
                    v.tensor_tensor(w_3[:, c], flat_a[1][:, 0, D * c:D * c + D], eye, ALU.add).then_inc(S_w3_rdy, 1)

            def layer2_residual(b):
                dve.wait_ge(S_x1b_rdy, 2 * b + 2)
                dve.wait_ge(S_l3_ps, 2 * b)
                for c in range(NC_):
                    dve.wait_ge(S_op_ps, 2 * b + c + 1)
                    v.scalar_tensor_tensor(x2[:, c], ps_p[:, c], dem_o[:, 1, c, b:b + 1], x1b[:, c],
                                           ALU.mult, ALU.add).then_inc(S_x2_rdy, 1)

            dve.wait_ge(S_con_in, 16)
            layer0_residual(0)
            demodulation_k(0)
            layer1_residual(0)
            keys(0, 0)
            keys(0, 1)
            dve.wait_ge(S_dec_in, 64)
            dve.wait_ge(S_ub_ps, 1)
            v.tensor_scalar(ub_sb[:], ps_q[0:RANK, 0, 0:B], bdec_sb[:, D:D + 1], None, ALU.add).then_inc(S_ub_added, 1)
            dve.wait_ge(S_b3_ps, 1)
            v.tensor_copy(bias3[:], ps_q[:, 0, 64:64 + NC_ * B].rearrange("p (c b) -> p c b", c=NC_)).then_inc(S_b3_rdy, 1)
            for b in range(1, B):
                gammas_down(b)
                demodulation_k(b)

            for b in range(B):
                nxt = b + 1 < B
                values(b, 0)
                values(b, 1)
                softmax_shift(b, 0)
                softmax_norm(b, 0)
                softmax_shift(b, 1)
                if nxt:
                    layer0_residual(b + 1)
                softmax_norm(b, 1)
                if nxt:
                    layer1_residual(b + 1)
                attention_out(b, 0)
                attention_out(b, 1)
                if nxt:
                    keys(b + 1, 0)
                    keys(b + 1, 1)
                layer3_weight(b)
                layer2_residual(b)

        @block.tensor
        def _(pe):
            mm = nc.tensor.matmul

            def gammas(b):
                pe.wait_ge(S_gbd_rdy, b)
                mm(ps_q[:, 1, P * b:P * b + P], cond_b[:, b], gbd_raw, start=True, stop=True).then_inc(S_gbd_ps, 1)
                mm(flat_a[b % 2][0:HID, b // 2], cond_b[:, b, 0:HID], gbu_raw, start=True, stop=True).then_inc(S_gbu_ps, 1)

            pe.wait_ge(S_par_in, 16)
            for l in range(MOD):
                for c in range(NC_):
                    n = l * NC_ + c
                    last = mm(ps_p[:, 1, B * n:B * n + B], aff[:, l, P * c:P * c + P], cond, start=True, stop=True)
            last.then_inc(S_style_ps, 1)
            pe.wait_ge(S_cond_rep, 1)
            pe.wait_ge(S_zeroed, 2)
            gammas(0)
            pe.wait_ge(S_squares, 1)
            pe.wait_ge(S_style_sq, 1)
            for i, l in enumerate((0, 2)):
                for h in range(NC_):
                    for c in range(NC_):
                        at = 64 + B * (NC_ * i + h)
                        last = mm(ps_p[:, 1, at:at + B], w_sq[:, l, c, P * h:P * h + P], style_sq[:, l, c],
                                  start=c == 0, stop=c == NC_ - 1)
            last.then_inc(S_varo_ps, 1)
            for c in range(NC_):
                last = mm(ps_q[0:B, 0, 0:D], style_sq[:, 1, c], w_sq[:, 1, c], start=c == 0, stop=c == NC_ - 1)
            last.then_inc(S_vark_ps, 1)

            def down(b):
                pe.wait_ge(S_x_in, 16 * b + 16)
                pe.wait_ge(S_wdown_rdy, b + 1)
                if b >= 2:
                    pe.wait_ge(S_x2_rdy, 2 * (b - 1))
                for c in range(NC_):
                    last = mm(ps_p[0:HID, 0], w_down[:, c], x_sb[:, b, c], start=c == 0, stop=c == NC_ - 1)
                last.then_inc(S_down_ps, 1)

            def layer3_weight(b):
                pe.wait_ge(S_u_added, 1)
                pe.wait_ge(S_ot_rdy, 2 * b + 1)
                for c in range(NC_):
                    last = mm(flat_a[1][:, 0, D * c:D * c + D], u_sb[:, b, P * c:P * c + P], v_sb[:], start=True, stop=True)
                last.then_inc(S_w3_ps, 1)

            def up(b):
                pe.wait_ge(S_hid_rdy, b + 1)
                pe.wait_ge(S_wup_rdy, b + 1)
                if b == 0:
                    pe.wait_ge(S_varo_in, 1)
                for c in range(NC_):
                    mm(ps_p[:, c], w_up[:, P * c:P * c + P], hid[:], start=True, stop=True).then_inc(S_up_ps, 1)

            def layer1(b):
                pe.wait_ge(S_wl1_rdy, 2 * b + 2)
                pe.wait_ge(S_x0_rdy, 2 * b + 2)
                if b == 0:
                    pe.wait_ge(S_demk_rdy, 1)
                for h in range(NC_):
                    if b >= 2:
                        pe.wait_ge(S_res_rdy, 2 * (b - 2) + h + 1)
                    for c in range(NC_):
                        last = mm(ps_q[:, h], w_l1[:, c, P * h:P * h + P], x0[:, c], start=c == 0, stop=c == NC_ - 1)
                    last.then_inc(S_l1_ps, 1)

            def keys(b, t):
                pe.wait_ge(S_wk_rdy, 2 * b + 2)
                pe.wait_ge(S_x1_rdy, 2 * b + 2)
                for u in range(U):
                    for c in range(NC_):
                        at = TOK * t + P * u
                        last = mm(ps_p[:, t, D * u:D * u + D], x1[:, c, at:at + P], w_k[:, c],
                                  start=c == 0, stop=c == NC_ - 1)
                last.then_inc(S_k_ps, 1)

            def scores(b, t):
                n = 2 * b + t
                pe.wait_ge(S_kTz_rdy, 2 * n + 2)
                if t == 0:
                    pe.wait_ge(S_ot_rdy, 2 * b)
                else:
                    pe.wait_ge(S_w3_rdy, 2 * b)
                for p in range(STRIP):
                    for g in range(G):
                        r = slice(STRIP * g, STRIP * g + STRIP)
                        last = mm(ps_a[t][STRIP * g:STRIP * g + NH, p // PL, :, p % PL], kT[t][r, :, p],
                                  kTz[t][r, :, :, p], start=True, stop=True)
                last.then_inc(S_s_ps, 1)

            def attend(b, t):
                n = 2 * b + t
                pe.wait_ge(S_pTz_rdy, 2 * n + 2)
                pe.wait_ge(S_vT_rdy, n + 1)
                pe.wait_ge(S_sc_rdy, 2 * b + 2 - t)
                for p in range(STRIP):
                    for g in range(G):
                        r = slice(STRIP * g, STRIP * g + STRIP)
                        last = mm(ps_a[1 - t][STRIP * g:STRIP * g + HD, p // PL, :, p % PL], vT[t][r, :, p],
                                  pTz[t][r, :, :, p], start=True, stop=True)
                last.then_inc(S_o_ps, 1)

            def transposes(b, nxt):
                pe.wait_ge(S_ot_rdy, 2 * b + 2)
                if nxt:
                    pe.wait_ge(S_y_rdy, 2 * b + 4)
                elif b:
                    pe.wait_ge(S_res_rdy, 2 * b)
                for h in range(NC_):
                    for t in range(TILES):
                        for u in range(U):
                            at = TOK * t + P * u
                            d = HD // NC_ * h
                            last = nc.tensor.transpose(ps_q[:, h, at:at + P], ot[t][:, u, d:d + HD // NC_].rearrange("p d h -> p (d h)"), ident)
                    last.then_inc(S_tr_ps, 1)

            def layer2_out(b, nxt):
                pe.wait_ge(S_wo_rdy, 2 * b + 2)
                pe.wait_ge(S_att_rdy, 2 * b + 2)
                if nxt:
                    pe.wait_ge(S_kx_rdy, 2 * b + 4)
                for h in range(NC_):
                    for c in range(NC_):
                        last = mm(ps_p[:, h], w_o[:, c, P * h:P * h + P], att[:, c], start=c == 0, stop=c == NC_ - 1)
                    last.then_inc(S_op_ps, 1)

            def layer3(b, h):
                pe.wait_ge(S_w3_rdy, 2 * b + 2)
                pe.wait_ge(S_x2_rdy, 2 * b + 2)
                for c in range(NC_):
                    last = mm(ps_q[:, h], w_3[:, c, P * h:P * h + P], x2[:, c], start=c == 0, stop=c == NC_ - 1)
                last.then_inc(S_l3_ps, 1)

            down(0)
            pe.wait_ge(S_con_in, 16)
            up(0)
            pe.wait_ge(S_normk_rdy, 1)
            mm(ps_q[:, 0, 0:D], pick[0], norm_k[:], start=True, stop=True).then_inc(S_demk_ps, 1)
            layer1(0)
            pe.wait_ge(S_dec_in, 64)
            pe.wait_ge(S_cond_pad, 1)
            pe.wait_ge(S_gbu_rdy, 1)
            for n in range(4):
                for g in range(G):
                    j = G * n + g
                    bank = flat_a[n % 2][STRIP * g:STRIP * g + STRIP, n // 2]
                    if j < NCH:
                        last = mm(bank, cond_z[:], wdec_sb[:, 2 * j:2 * j + 2], start=True, stop=True)
                last.then_inc(S_urow_ps, 1)
            keys(0, 0)
            keys(0, 1)
            mm(ps_q[0:RANK, 0, 0:B], wdecb_sb[:], cond, start=True, stop=True).then_inc(S_ub_ps, 1)
            pe.wait_ge(S_ub_added, 1)
            for h in range(NC_):
                last = mm(ps_q[:, 0, 64 + B * h:64 + B * h + B], v_sb[:, P * h:P * h + P], ub_sb[:], start=True, stop=True)
            last.then_inc(S_b3_ps, 1)
            for b in range(1, B):
                pe.wait_ge(S_urow_rdy, 4)
                gammas(b)
                if b >= 2:
                    pe.wait_ge(S_demk_rdy, b)
                mm(flat_a[0][:, 0, 0:D], pick[b], norm_k[:], start=True, stop=True).then_inc(S_demk_ps, 1)
            pe.wait_ge(S_gbu_rdy, B)
            pe.wait_ge(S_gbd_rdy, B)
            pe.wait_ge(S_demk_rdy, B)
            pe.wait_ge(S_b3_rdy, 1)

            for b in range(B):
                nxt = b + 1 < B
                scores(b, 0)
                scores(b, 1)
                if nxt:
                    down(b + 1)
                if b:
                    layer3(b - 1, 0)
                if nxt:
                    up(b + 1)
                if b:
                    layer3(b - 1, 1)
                if nxt:
                    layer1(b + 1)
                attend(b, 0)
                attend(b, 1)
                if nxt:
                    keys(b + 1, 0)
                    keys(b + 1, 1)
                transposes(b, nxt)
                layer3_weight(b)
                layer2_out(b, nxt)
            layer3(B - 1, 0)
            layer3(B - 1, 1)


def kernel(x, cond_512, L0_cond_down_project, L0_cond_down_gamma, L0_cond_down_beta,
           L0_cond_up_project, L0_cond_up_gamma, L0_cond_up_beta, L1_cond_weight, L1_cond_bias,
           L1_cond_affine_w, L1_cond_affine_b, L2_cond_k_aff_w, L2_cond_k_aff_b, L2_cond_k_w,
           L2_cond_k_b, L2_cond_o_aff_w, L2_cond_o_aff_b, L2_cond_o_w, L2_cond_o_b, L3_cond_W_dec,
           L3_cond_b_dec, L3_cond_V):
    import concourse.bacc as bacc
    from concourse.bass_utils import run_bass_kernel_spmd

    def halves(a):
        a = np.asarray(a).reshape(NC_, P, -1)
        return a.transpose(1, 0, 2).reshape(P, -1)

    def by_dim(a):
        a = np.asarray(a)
        return a.reshape((NH, HD) + a.shape[1:]).swapaxes(0, 1).reshape(a.shape)

    up = np.zeros((P, D), np.float32)
    up[:HID] = np.asarray(L0_cond_up_project)
    params = np.concatenate(
        [np.asarray(cond_512).T]
        + [halves(a) for a in (L1_cond_affine_b, L2_cond_k_aff_b, by_dim(L2_cond_o_aff_b), L1_cond_bias, L2_cond_o_b)]
        + [np.asarray(a).T for a in (L1_cond_affine_w, L2_cond_k_aff_w, by_dim(L2_cond_o_aff_w))]
        + [halves(L0_cond_down_project)]
        + [np.asarray(a) for a in (L0_cond_down_gamma, L0_cond_down_beta, L0_cond_up_gamma, L0_cond_up_beta)]
        + [up], axis=1)
    weights = np.stack([halves(np.asarray(a).T) for a in (L1_cond_weight, L2_cond_k_w)]
                       + [halves(by_dim(np.asarray(L2_cond_o_w).T))], axis=1)
    wdec = np.asarray(L3_cond_W_dec).reshape(C, D + 1, RANK).transpose(0, 2, 1)
    eye = np.zeros((P, CONSTW), np.float32)
    eye[:, P:2 * P] = np.eye(P)
    for b in range(B):
        eye[b, 3 * P + U + P * b:3 * P + U + P * b + P] = 1.0
    for u in range(U):
        eye[:, 3 * P + u] = np.arange(P) % STRIP // (STRIP // U) == u
    arrays = {
        "xT": np.asarray(x).reshape(B, S, NC_, P).transpose(3, 0, 2, 1),
        "params": params,
        "weights": weights.reshape(P, MOD, NC_, D),
        "kb": np.asarray(L2_cond_k_b).reshape(1, D),
        "wdec": wdec[:, :, :D],
        "wdecb": wdec[:, :, D],
        "bdec": np.asarray(L3_cond_b_dec).reshape(D + 1, RANK).T,
        "vmat": np.asarray(L3_cond_V),
        "consts": eye,
    }
    arrays = {k: np.ascontiguousarray(a) for k, a in arrays.items()}
    nc = bacc.Bacc("TRN2", target_bir_lowering=False, num_devices=1)
    args = [nc.dram_tensor(k, a.shape, mybir.dt.from_np(a.dtype), kind="ExternalInput").ap() for k, a in arrays.items()]
    out = nc.dram_tensor("outT", (P, B, NC_, S), mybir.dt.float32, kind="ExternalOutput").ap()
    cond_resid_kernel(nc, *args, out)
    r = run_bass_kernel_spmd(nc, [arrays], core_ids=[0])
    got = r.results[0]["outT"]
    return np.ascontiguousarray(got.transpose(1, 3, 2, 0).reshape(B, S, D))
```

```python
import numpy as np

import concourse.bass as bass
from concourse import mybir

B, S, D, C = 4, 512, 256, 128
HID = 64
NH, HD = 16, 16
RANK = 30
P = 128
NC_ = D // P
TILES = 2
TOK = S // TILES
U = 2
STRIP = 32
G = P // STRIP
PL = STRIP // 2
MOD = 3
CHUNK = 2 * D
NCH = RANK // 2
AT_VAR = P + D
AT_UB = slice(0, B)
AT_B3 = B
GAIN = float(1.0 / np.sqrt(C).astype(np.float32))
EPS = 1e-8
CLAMP = 256.0

PAR = {}
_at = 0
for _n, _w in (("cond", B), ("affb", MOD * NC_), ("outb", 2 * NC_), ("aff", MOD * D),
               ("down", NC_ * HID), ("gbdown", 2 * HID), ("gbup", 2 * D), ("up", D)):
    PAR[_n] = slice(_at, _at + _w)
    _at += _w
PARW = _at
CONSTW = 3 * P + U


def cond_resid_kernel(nc, xT, params, weights, kb, wdec, wdecb, bdec, vmat, consts, picks, outT):
    f32 = mybir.dt.float32
    ALU = mybir.AluOpType
    ACT = mybir.ActivationFunctionType
    AX = mybir.AxisListType
    from contextlib import ExitStack

    ctx = ExitStack()
    with ctx:
        def sb(name, shape):
            return ctx.enter_context(nc.sbuf_tensor(name, shape, f32))

        def sem(name):
            return ctx.enter_context(nc.semaphore(name))

        par = sb("par", [P, PARW])
        w_raw = sb("w_raw", [P, MOD, NC_, D])
        w_sq = sb("w_sq", [P, MOD, NC_, D])
        kb_b = sb("kb_b", [P, NH, HD])
        wdec_sb = sb("wdec_sb", [P, RANK, D])
        wdecb_sb = sb("wdecb_sb", [P, RANK])
        bdec_sb = sb("bdec_sb", [RANK, D + 1])
        v_sb = sb("v_sb", [P, G, D])
        con = sb("con", [P, CONSTW])
        picks_sb = sb("picks_sb", [B, B, P])
        x_sb = sb("x_sb", [P, B, NC_, S])
        cond_b = sb("cond_b", [P, B, P])
        cond_z = sb("cond_z", [P, STRIP])
        style = sb("style", [P, MOD, NC_, B])
        style_sq = sb("style_sq", [P, MOD, NC_, B])
        var_k = sb("var_k", [B, D])
        root_k = sb("root_k", [B, D])
        rec_k = sb("rec_k", [B, D])
        corr_k = sb("corr_k", [B, D])
        norm_k = sb("norm_k", [B, D])
        dem_k = sb("dem_k", [P, B, D])
        var_o = sb("var_o", [P, 2, NC_, B])
        root_o = sb("root_o", [P, 2, NC_, B])
        rec_o = sb("rec_o", [P, 2, NC_, B])
        corr_o = sb("corr_o", [P, 2, NC_, B])
        dem_o = sb("dem_o", [P, 2, NC_, B])
        gb_down = sb("gb_down", [P, B, 2, HID])
        gb_up = sb("gb_up", [P, B, 2, D])
        urow = sb("urow", [P, 4, 2, D])
        u_rows = sb("u_rows", [RANK, B, D])
        u_sb = sb("u_sb", [P, NC_, B, STRIP])
        ub_sb = sb("ub_sb", [RANK, B])
        bias3 = sb("bias3", [P, NC_, B])
        w_down = sb("w_down", [P, NC_, HID])
        w_up = sb("w_up", [P, D])
        w_l1 = sb("w_l1", [P, NC_, D])
        w_k = sb("w_k", [P, NC_, D])
        w_o = sb("w_o", [P, NC_, D])
        hid = sb("hid", [P, 2, S // 2])
        x0 = sb("x0", [P, NC_, S])
        y1 = sb("y1", [P, NC_, S])
        x1 = sb("x1", [P, NC_, S])
        x1b = sb("x1b", [P, NC_, S])
        x2 = sb("x2", [P, NC_, S])
        att = sb("att", [P, NC_, S])
        xu = sb("xu", [P, S // G])
        res = sb("res", [P, NC_, S])
        kx = [sb(f"kx{t}", [P, U, NH, HD]) for t in range(TILES)]
        kT = [sb(f"kT{t}", [P, NH, STRIP]) for t in range(TILES)]
        kTz = [sb(f"kTz{t}", [P, U, NH, STRIP]) for t in range(TILES)]
        vT = [sb(f"vT{t}", [P, HD, STRIP]) for t in range(TILES)]
        sc = sb("sc", [P, U * NH, STRIP])
        mx = sb("mx", [P, U * NH])
        sh = sb("sh", [P, U * NH, NH])
        ex = sb("ex", [P, U * NH, NH])
        zs = sb("zs", [P, U * NH])
        rz = sb("rz", [P, U * NH])
        pn = sb("pn", [P, U * NH, NH])
        pT = sb("pT", [P, NH, STRIP])
        pTz = [sb(f"pTz{t}", [P, U, NH, STRIP]) for t in range(TILES)]
        ot = [sb(f"ot{t}", [P, U, STRIP, NH]) for t in range(TILES)]

        urow_d = nc.dram_tensor("urow_d", [B, 4, G, 2, D], f32, kind="Internal").ap()

        ps_a = [ctx.enter_context(nc.psum_tensor(f"ps_a{i}", [P, 2, U * NH, PL], f32)) for i in range(2)]
        ps_p = ctx.enter_context(nc.psum_tensor("ps_p", [P, 2, S], f32))
        ps_q = ctx.enter_context(nc.psum_tensor("ps_q", [P, 2, S], f32))

        pick = [picks_sb[:, b] for b in range(B)]
        flat_a = [a[:].rearrange("p b m l -> p b (m l)") for a in ps_a]
        ident = con[:, P:2 * P]
        half = [con[:, 3 * P + u:3 * P + u + 1] for u in range(U)]
        cond = par[:, PAR["cond"]]
        affb = par[:, PAR["affb"]]
        outb = par[:, PAR["outb"]]
        aff = par[:, PAR["aff"]].rearrange("p (l i) -> p l i", l=MOD)
        wd_raw = par[:, PAR["down"]].rearrange("p (c h) -> p c h", c=NC_)
        gbd_raw = par[:, PAR["gbdown"]]
        gbu_raw = par[:, PAR["gbup"]]
        wu_raw = par[:, PAR["up"]]

        S_aff_in = sem("aff_in")
        S_par_in = sem("par_in")
        S_w_in = sem("w_in")
        S_kb_in = sem("kb_in")
        S_con_in = sem("con_in")
        S_pick_in = sem("pick_in")
        S_padded = sem("padded")
        S_dec_in = sem("dec_in")
        S_x_in = sem("x_in")
        S_out_dma = sem("out_dma")
        S_ur_out = sem("ur_out")
        S_ur_in = sem("ur_in")
        S_zeroed = sem("zeroed")
        S_cond_rep = sem("cond_rep")
        S_cond_pad = sem("cond_pad")
        S_style_ps = sem("style_ps")
        S_styled = sem("styled")
        S_squares = sem("squares")
        S_style_sq = sem("style_sq")
        S_varo_ps = sem("varo_ps")
        S_vark_ps = sem("vark_ps")
        S_varo_in = sem("varo_in")
        S_vark_in = sem("vark_in")
        S_rooto_rdy = sem("rooto_rdy")
        S_rootk_rdy = sem("rootk_rdy")
        S_demo_step = sem("demo_step")
        S_demk_step = sem("demk_step")
        S_demo_rdy = sem("demo_rdy")
        S_normk_rdy = sem("normk_rdy")
        S_demk_ps = sem("demk_ps")
        S_demk_rdy = sem("demk_rdy")
        S_gbd_ps = sem("gbd_ps")
        S_gbd_rdy = sem("gbd_rdy")
        S_gbu_ps = sem("gbu_ps")
        S_gbu_rdy = sem("gbu_rdy")
        S_urow_ps = sem("urow_ps")
        S_u_ps = sem("u_ps")
        S_u_rdy = sem("u_rdy")
        S_urow_rdy = sem("urow_rdy")
        S_u_added = sem("u_added")
        S_ub_added = sem("ub_added")
        S_ub_ps = sem("ub_ps")
        S_b3_ps = sem("b3_ps")
        S_b3_rdy = sem("b3_rdy")
        S_wdown_scaled = sem("wdown_scaled")
        S_wup_scaled = sem("wup_scaled")
        S_wk_scaled = sem("wk_scaled")
        S_wdown_rdy = sem("wdown_rdy")
        S_wup_rdy = sem("wup_rdy")
        S_wl1_rdy = sem("wl1_rdy")
        S_wk_rdy = sem("wk_rdy")
        S_wo_rdy = sem("wo_rdy")
        S_down_ps = sem("down_ps")
        S_hid_rdy = sem("hid_rdy")
        S_up_ps = sem("up_ps")
        S_x0_rdy = sem("x0_rdy")
        S_l1_ps = sem("l1_ps")
        S_y_rdy = sem("y_rdy")
        S_clipped = sem("clipped")
        S_x1_rdy = sem("x1_rdy")
        S_x1b_rdy = sem("x1b_rdy")
        S_k_ps = sem("k_ps")
        S_kx_rdy = sem("kx_rdy")
        S_kT_rdy = sem("kT_rdy")
        S_kTz_rdy = sem("kTz_rdy")
        S_vT_rdy = sem("vT_rdy")
        S_s_ps = sem("s_ps")
        S_sc_rdy = sem("sc_rdy")
        S_mx_rdy = sem("mx_rdy")
        S_sh_rdy = sem("sh_rdy")
        S_ex_rdy = sem("ex_rdy")
        S_zs_rdy = sem("zs_rdy")
        S_rz_rdy = sem("rz_rdy")
        S_pn_rdy = sem("pn_rdy")
        S_pT_rdy = sem("pT_rdy")
        S_pTz_rdy = sem("pTz_rdy")
        S_o_ps = sem("o_ps")
        S_ot_rdy = sem("ot_rdy")
        S_tr_ps = sem("tr_ps")
        S_att_rdy = sem("att_rdy")
        S_op_ps = sem("op_ps")
        S_x2_rdy = sem("x2_rdy")
        S_xu_ps = sem("xu_ps")
        S_xu_rdy = sem("xu_rdy")
        S_l3_ps = sem("l3_ps")
        S_res_rdy = sem("res_rdy")

        block = ctx.enter_context(nc.Block())

        @block.sync
        def _(sp):
            first = PAR["aff"].stop
            sp.dma_start(par[:, 0:first], params[:, 0:first]).then_inc(S_aff_in, 16)
            sp.dma_start(par[:, first:], params[:, first:]).then_inc(S_par_in, 16)
            sp.dma_start(x_sb[:, 0], xT[:, 0]).then_inc(S_x_in, 16)
            sp.dma_start(wdec_sb[:], wdec).then_inc(S_dec_in, 16)
            sp.dma_start(wdecb_sb[:], wdecb).then_inc(S_dec_in, 16)
            sp.dma_start(bdec_sb[:], bdec).then_inc(S_dec_in, 16)
            sp.wait_ge(S_padded, 1)
            for q in range(G):
                sp.dma_start(v_sb[STRIP * q:STRIP * q + RANK, q], vmat).then_inc(S_dec_in, 16)
            for b in range(1, B):
                sp.wait_ge(S_x_in, 16 * b)
                sp.dma_start(x_sb[:, b], xT[:, b]).then_inc(S_x_in, 16)
            sp.wait_ge(S_urow_rdy, 4)
            for g in range(G):
                slots = 4 if 3 * G + g < NCH else 3
                sp.dma_start(urow_d[:, 0:slots, g], urow[STRIP * g:STRIP * g + B, 0:slots]).then_inc(S_ur_out, 16)
            sp.wait_ge(S_ur_out, 16 * G)
            sp.dma_start(u_rows[:], urow_d.rearrange("b n g k i -> (n g k) b i")[0:RANK]).then_inc(S_ur_in, 16)

            for b in range(B):
                sp.wait_ge(S_res_rdy, 2 * b + 2)
                sp.dma_start(outT[:, b], res[:]).then_inc(S_out_dma, 16)
            sp.wait_ge(S_out_dma, 16 * B)

        @block.gpsimd
        def _(pool):
            def weights_down_up(b):
                pool.wait_ge(S_gbd_rdy, b + 1)
                pool.wait_ge(S_down_ps, b)
                gd = gb_down[:, b, 0:1].to_broadcast([P, NC_, HID])
                bd = gb_down[:, b, 1:2].to_broadcast([P, NC_, HID])
                pool.tensor_tensor(w_down[:], wd_raw, gd, ALU.mult).then_inc(S_wdown_scaled, 1)
                pool.wait_ge(S_wdown_scaled, b + 1)
                pool.tensor_tensor(w_down[:], w_down[:], bd, ALU.add).then_inc(S_wdown_rdy, 1)
                pool.wait_ge(S_gbu_rdy, b + 1)
                pool.wait_ge(S_up_ps, 2 * b)
                pool.tensor_tensor(w_up[:], wu_raw, gb_up[:, b, 0], ALU.mult).then_inc(S_wup_scaled, 1)
                pool.wait_ge(S_wup_scaled, b + 1)
                pool.tensor_tensor(w_up[:], w_up[:], gb_up[:, b, 1], ALU.add).then_inc(S_wup_rdy, 1)

            def weights_l1_k(b):
                pool.wait_ge(S_styled, 6)
                pool.wait_ge(S_l1_ps, 2 * b)
                for c in range(NC_):
                    pool.tensor_scalar(w_l1[:, c], w_raw[:, 0, c], style[:, 0, c, b:b + 1], 1.0,
                                       ALU.mult, ALU.mult).then_inc(S_wl1_rdy, 1)
                pool.wait_ge(S_k_ps, 2 * b)
                for c in range(NC_):
                    pool.tensor_scalar(w_k[:, c], w_raw[:, 1, c], style[:, 1, c, b:b + 1], 1.0,
                                       ALU.mult, ALU.mult).then_inc(S_wk_scaled, 1)
                pool.wait_ge(S_demk_rdy, b + 1)
                for c in range(NC_):
                    pool.wait_ge(S_wk_scaled, 2 * b + c + 1)
                    pool.tensor_tensor(w_k[:, c], w_k[:, c], dem_k[:, b], ALU.mult).then_inc(S_wk_rdy, 1)

            def weights_o(b):
                pool.wait_ge(S_op_ps, 2 * b)
                for c in range(NC_):
                    pool.tensor_scalar(w_o[:, c], w_raw[:, 2, c], style[:, 2, c, b:b + 1], 1.0,
                                       ALU.mult, ALU.mult).then_inc(S_wo_rdy, 1)

            def residual_bias(b):
                pool.wait_ge(S_x1_rdy, 2 * b + 2)
                pool.wait_ge(S_x2_rdy, 2 * b)
                for c in range(NC_):
                    pool.tensor_scalar(x1b[:, c], x1[:, c], 1.0, outb[:, NC_ + c:NC_ + c + 1],
                                       ALU.mult, ALU.add).then_inc(S_x1b_rdy, 1)

            pool.memset(v_sb[:], 0.0).then_inc(S_padded, 1)
            pool.memset(hid[:], 0.0).then_inc(S_padded, 1)
            pool.wait_ge(S_par_in, 16)
            weights_down_up(0)
            pool.wait_ge(S_w_in, 16)
            weights_l1_k(0)
            pool.wait_ge(S_dec_in, 16 * (3 + G))
            residual_bias(0)
            pool.wait_ge(S_ur_in, 16)
            pool.tensor_tensor(u_rows[:], u_rows[:], bdec_sb[:, 0:D].rearrange("k (o i) -> k o i", o=1).to_broadcast([RANK, B, D]),
                               ALU.add).then_inc(S_u_added, 1)

            def batch(b, nxt):
                if nxt:
                    weights_down_up(b + 1)
                    weights_l1_k(b + 1)
                weights_o(b)
                if nxt:
                    residual_bias(b + 1)

            for b in range(B):
                batch(b, b + 1 < B)

        @block.scalar
        def _(act):
            act.dma_start(w_raw[:], weights).then_inc(S_w_in, 16)
            act.dma_start(picks_sb[:], picks).then_inc(S_pick_in, 16)
            act.dma_start(con[:], consts).then_inc(S_con_in, 16)
            act.dma_start(kb_b[:], kb.to_broadcast([P, D]).rearrange("p (h d) -> p h d", h=NH)).then_inc(S_kb_in, 16)

            def gammas_up(b):
                act.wait_ge(S_gbu_ps, b + 1)
                nc.scalar.activation(gb_up[:, b].rearrange("h g i -> h (g i)"), ps_q[:, 0],
                                     ACT.Copy).then_inc(S_gbu_rdy, 1)

            def squares(first, end):
                act.wait_ge(S_w_in, 16)
                nc.scalar.activation(w_sq[:, first:end:2], w_raw[:, first:end:2], ACT.Square).then_inc(S_squares, 1)

            def root_out():
                act.wait_ge(S_varo_in, 1)
                nc.scalar.activation(root_o[:], var_o[:], ACT.Sqrt).then_inc(S_rooto_rdy, 1)

            def root_key():
                act.wait_ge(S_vark_in, 1)
                nc.scalar.activation(root_k[:], var_k[:], ACT.Sqrt).then_inc(S_rootk_rdy, 1)

            def relu(b):
                act.wait_ge(S_down_ps, b + 1)
                act.wait_ge(S_up_ps, 2 * b)
                act.wait_ge(S_padded, 2)
                for g in range(2):
                    r = slice(HID * g, HID * g + HID)
                    nc.scalar.activation(hid[r, g], ps_p[r, 0, 0:S // 2], ACT.Relu).then_inc(S_hid_rdy, 1)

            def demodulate(b, c):
                act.wait_ge(S_demo_rdy, 1)
                act.wait_ge(S_l1_ps, 2 * b + c + 1)
                act.wait_ge(S_x1_rdy, 2 * b)
                nc.scalar.activation(y1[:, c], ps_q[:, c], ACT.Identity, bias=outb[:, c:c + 1],
                                     scale=dem_o[:, 0, c, b:b + 1]).then_inc(S_y_rdy, 1)

            def exponentials(b, t):
                act.wait_ge(S_sh_rdy, 2 * b + t + 1)
                act.wait_ge(S_pn_rdy, 2 * b + t)
                nc.scalar.activation(ex[:], sh[:], ACT.Exp, scale=HD ** -0.5).then_inc(S_ex_rdy, 1)

            def attention_copy(b):
                act.wait_ge(S_op_ps, 2 * b)
                for c in range(NC_):
                    act.wait_ge(S_tr_ps, 2 * b + c + 1)
                    nc.scalar.activation(att[:, c], ps_q[:, c], ACT.Copy).then_inc(S_att_rdy, 1)

            def copy_xu(b):
                act.wait_ge(S_xu_ps, b + 1)
                act.wait_ge(S_l3_ps, 2 * b)
                nc.scalar.activation(xu[:], ps_q[:, 0, 0:S // G], ACT.Copy).then_inc(S_xu_rdy, 1)

            def copy_rows(n):
                act.wait_ge(S_urow_ps, n + 1)
                nc.scalar.activation(urow[:, n].rearrange("p k i -> p (k i)"), flat_a[n % 2][:, n // 2],
                                     ACT.Copy).then_inc(S_urow_rdy, 1)

            squares(1, 2)
            squares(0, 3)
            gammas_up(0)
            root_key()
            relu(0)
            root_out()
            demodulate(0, 0)
            demodulate(0, 1)
            copy_rows(0)
            gammas_up(1)
            copy_rows(1)
            copy_rows(2)
            copy_rows(3)
            for b in range(2, B):
                gammas_up(b)

            for b in range(B):
                if b > 0:
                    attention_copy(b - 1)
                exponentials(b, 0)
                if b > 0:
                    copy_xu(b - 1)
                if b + 1 < B:
                    relu(b + 1)
                exponentials(b, 1)
                if b + 1 < B:
                    demodulate(b + 1, 0)
                    demodulate(b + 1, 1)
            attention_copy(B - 1)
            copy_xu(B - 1)

        @block.vector
        def _(dve):
            v = nc.vector
            for a in ps_a:
                v.memset(a[:], 0.0).then_inc(S_zeroed, 1)
            v.memset(cond_z[:], 0.0).then_inc(S_zeroed, 1)
            v.memset(u_sb[:], 0.0).then_inc(S_zeroed, 1)
            dve.wait_ge(S_aff_in, 16)
            v.tensor_copy(cond_b[:], cond.rearrange("p (b o) -> p b o", o=1).to_broadcast([P, B, P])).then_inc(S_cond_rep, 1)
            dve.wait_ge(S_style_ps, 1)
            for l in range(MOD):
                for c in range(NC_):
                    n = l * NC_ + c
                    v.tensor_scalar(style[:, l, c], ps_p[:, 1, B * n:B * n + B], GAIN if l == 0 else 1.0,
                                    affb[:, n:n + 1], ALU.mult, ALU.add).then_inc(S_styled, 1)
            dve.wait_ge(S_styled, 6)
            v.tensor_tensor(style_sq[:], style[:], style[:], ALU.mult).then_inc(S_style_sq, 1)

            def gammas_down(b):
                dve.wait_ge(S_gbd_ps, b + 1)
                v.tensor_copy(gb_down[:, b].rearrange("p g h -> p (g h)"), ps_q[:, 1, 0:P]).then_inc(S_gbd_rdy, 1)

            gammas_down(0)
            dve.wait_ge(S_zeroed, 3)
            v.tensor_copy(cond_z[:, 0:B], cond).then_inc(S_cond_pad, 1)

            def variances_out():
                dve.wait_ge(S_varo_ps, 1)
                v.tensor_scalar(var_o[:].rearrange("p l c b -> p (l c b)"), ps_q[:, 1, AT_VAR:AT_VAR + 2 * NC_ * B], EPS, None,
                                ALU.add).then_inc(S_varo_in, 1)

            def variances_key():
                dve.wait_ge(S_vark_ps, 1)
                v.tensor_scalar(var_k[:], ps_q[0:B, 0, 0:D], EPS, None, ALU.add).then_inc(S_vark_in, 1)

            def newton_out():
                dve.wait_ge(S_rooto_rdy, 1)
                v.reciprocal(rec_o[:], root_o[:]).then_inc(S_demo_step, 1)
                dve.wait_ge(S_demo_step, 1)
                v.tensor_tensor(corr_o[:], rec_o[:], rec_o[:], ALU.mult).then_inc(S_demo_step, 1)
                dve.wait_ge(S_demo_step, 2)
                v.tensor_tensor(corr_o[:], corr_o[:], var_o[:], ALU.mult).then_inc(S_demo_step, 1)
                dve.wait_ge(S_demo_step, 3)
                v.tensor_scalar(corr_o[:], corr_o[:], -0.5, 1.5, ALU.mult, ALU.add).then_inc(S_demo_step, 1)
                dve.wait_ge(S_demo_step, 4)
                v.tensor_tensor(dem_o[:], rec_o[:], corr_o[:], ALU.mult).then_inc(S_demo_rdy, 1)

            def newton_key():
                dve.wait_ge(S_rootk_rdy, 1)
                v.reciprocal(rec_k[:], root_k[:]).then_inc(S_demk_step, 1)
                dve.wait_ge(S_demk_step, 1)
                v.tensor_tensor(corr_k[:], rec_k[:], rec_k[:], ALU.mult).then_inc(S_demk_step, 1)
                dve.wait_ge(S_demk_step, 2)
                v.tensor_tensor(corr_k[:], corr_k[:], var_k[:], ALU.mult).then_inc(S_demk_step, 1)
                dve.wait_ge(S_demk_step, 3)
                v.tensor_scalar(corr_k[:], corr_k[:], -0.5, 1.5, ALU.mult, ALU.add).then_inc(S_demk_step, 1)
                dve.wait_ge(S_demk_step, 4)
                v.tensor_tensor(norm_k[:], rec_k[:], corr_k[:], ALU.mult).then_inc(S_normk_rdy, 1)

            def demodulation_k(b):
                dve.wait_ge(S_demk_ps, b + 1)
                v.tensor_copy(dem_k[:, b], ps_q[:, 1, P:P + D] if b else flat_a[1][:, 1, 0:D]).then_inc(S_demk_rdy, 1)

            def layer0_residual(b):
                dve.wait_ge(S_x_in, 16 * b + 16)
                dve.wait_ge(S_l1_ps, 2 * b)
                for g in range(2):
                    dve.wait_ge(S_up_ps, 2 * b + g + 1)
                    tok = slice(S // 2 * g, S // 2 * g + S // 2)
                    v.scalar_tensor_tensor(x0[:, :, tok], x_sb[:, b, :, tok], 2.0,
                                           ps_p[:, g].rearrange("p (c n) -> p c n", c=NC_), ALU.mult, ALU.add).then_inc(S_x0_rdy, 1)

            def layer1_residual(b):
                dve.wait_ge(S_k_ps, 2 * b)
                dve.wait_ge(S_x1b_rdy, 2 * b)
                for c in range(NC_):
                    dve.wait_ge(S_y_rdy, 2 * b + c + 1)
                    v.tensor_scalar(y1[:, c], y1[:, c], -CLAMP, CLAMP, ALU.max, ALU.min).then_inc(S_clipped, 1)
                    dve.wait_ge(S_clipped, 2 * b + c + 1)
                    v.tensor_tensor(x1[:, c], x0[:, c], y1[:, c], ALU.add).then_inc(S_x1_rdy, 1)

            def keys(b, t):
                n = 2 * b + t
                dve.wait_ge(S_k_ps, n + 1)
                dve.wait_ge(S_kb_in, 16)
                dve.wait_ge(S_con_in, 16)
                v.tensor_tensor(kx[t][:], ps_p[:, t].rearrange("p (u h d) -> p u h d", u=U, h=NH),
                                kb_b[:].rearrange("p (o h) d -> p o h d", o=1).to_broadcast([P, U, NH, HD]), ALU.add).then_inc(S_kx_rdy, 1)
                dve.wait_ge(S_kx_rdy, n + 1)
                dve.wait_ge(S_s_ps, 2 * b)
                v.transpose(kT[t][:], kx[t][:].rearrange("p u h d -> p h u d")).then_inc(S_kT_rdy, 1)
                dve.wait_ge(S_kT_rdy, n + 1)
                for u in range(U):
                    v.tensor_scalar(kTz[t][:, u], kT[t][:], half[u], None, ALU.mult).then_inc(S_kTz_rdy, 1)

            def values(b, t):
                n = 2 * b + t
                dve.wait_ge(S_o_ps, 2 * b)
                v.transpose(vT[t][:], kx[t][:].rearrange("p u j d -> p d u j")).then_inc(S_vT_rdy, 1)

            def softmax_shift(b, t):
                n = 2 * b + t
                dve.wait_ge(S_s_ps, n + 1)
                v.transpose(sc[:], ps_a[t][:].rearrange("p b m l -> p m b l")).then_inc(S_sc_rdy, 1)
                dve.wait_ge(S_sc_rdy, n + 1)
                v.reduce_max(mx[:], sc[:, :, 0:NH], AX.X).then_inc(S_mx_rdy, 1)
                dve.wait_ge(S_mx_rdy, n + 1)
                v.tensor_tensor(sh[:], sc[:, :, 0:NH],
                                mx[:].rearrange("p (m o) -> p m o", o=1).to_broadcast([P, U * NH, NH]),
                                ALU.subtract).then_inc(S_sh_rdy, 1)

            def softmax_norm(b, t):
                n = 2 * b + t
                dve.wait_ge(S_ex_rdy, n + 1)
                v.reduce_sum(zs[:], ex[:], AX.X).then_inc(S_zs_rdy, 1)
                dve.wait_ge(S_zs_rdy, n + 1)
                v.reciprocal(rz[:], zs[:]).then_inc(S_rz_rdy, 1)
                dve.wait_ge(S_rz_rdy, n + 1)
                v.tensor_tensor(pn[:], ex[:], rz[:].rearrange("p (m o) -> p m o", o=1).to_broadcast([P, U * NH, NH]),
                                ALU.mult).then_inc(S_pn_rdy, 1)
                dve.wait_ge(S_pn_rdy, n + 1)
                v.transpose(pT[:], pn[:].rearrange("p (u h) j -> p h u j", u=U)).then_inc(S_pT_rdy, 1)
                dve.wait_ge(S_pT_rdy, n + 1)
                dve.wait_ge(S_o_ps, 2 * b)
                for u in range(U):
                    v.tensor_scalar(pTz[t][:, u], pT[:], half[u], None, ALU.mult).then_inc(S_pTz_rdy, 1)

            def attention_out(b, t):
                n = 2 * b + t
                dve.wait_ge(S_o_ps, n + 1)
                dve.wait_ge(S_tr_ps, 2 * b)
                v.transpose(ot[t][:].rearrange("p u d h -> p u h d"),
                            ps_a[t][:].rearrange("p b m l -> p m b l")).then_inc(S_ot_rdy, 1)

            def generated_u():
                dve.wait_ge(S_u_ps, 1)
                dve.wait_ge(S_zeroed, 4)
                got = ps_q[:, 1, 0:NC_ * B * STRIP].rearrange("p (c b k) -> p c b k", c=NC_, b=B)
                v.tensor_copy(u_sb[:, :, :, 0:RANK], got[:, :, :, 0:RANK]).then_inc(S_u_rdy, 1)

            def layer3_residual(b, c):
                dve.wait_ge(S_b3_rdy, 1)
                dve.wait_ge(S_out_dma, 16 * b)
                dve.wait_ge(S_l3_ps, 2 * b + c + 1)
                v.scalar_tensor_tensor(res[:, c], ps_q[:, c], bias3[:, c, b:b + 1], x2[:, c],
                                       ALU.add, ALU.add).then_inc(S_res_rdy, 1)

            def layer2_residual(b):
                dve.wait_ge(S_x1b_rdy, 2 * b + 2)
                dve.wait_ge(S_res_rdy, 2 * b)
                for c in range(NC_):
                    dve.wait_ge(S_op_ps, 2 * b + c + 1)
                    v.scalar_tensor_tensor(x2[:, c], ps_p[:, c], dem_o[:, 1, c, b:b + 1], x1b[:, c],
                                           ALU.mult, ALU.add).then_inc(S_x2_rdy, 1)

            def layer3_bias_rows():
                dve.wait_ge(S_dec_in, 16 * (3 + G))
                dve.wait_ge(S_ub_ps, 1)
                v.tensor_scalar(ub_sb[:], flat_a[1][0:RANK, 0, AT_UB], bdec_sb[:, D:D + 1], None, ALU.add).then_inc(S_ub_added, 1)

            def layer3_bias():
                dve.wait_ge(S_b3_ps, 1)
                v.tensor_copy(bias3[:], flat_a[1][:, 0, AT_B3:AT_B3 + NC_ * B].rearrange("p (c b) -> p c b", c=NC_)).then_inc(S_b3_rdy, 1)

            variances_key()
            variances_out()
            layer0_residual(0)
            newton_key()
            newton_out()
            demodulation_k(0)
            layer1_residual(0)
            keys(0, 0)
            keys(0, 1)
            gammas_down(1)
            demodulation_k(1)
            layer3_bias_rows()
            layer3_bias()
            for b in range(2, B):
                gammas_down(b)
                demodulation_k(b)

            for b in range(B):
                values(b, 0)
                if b > 0:
                    layer2_residual(b - 1)
                softmax_shift(b, 0)
                if b == 1:
                    generated_u()
                softmax_norm(b, 0)
                softmax_shift(b, 1)
                if b > 0:
                    layer3_residual(b - 1, 0)
                if b + 1 < B:
                    layer0_residual(b + 1)
                values(b, 1)
                if b > 0:
                    layer3_residual(b - 1, 1)
                softmax_norm(b, 1)
                if b + 1 < B:
                    layer1_residual(b + 1)
                attention_out(b, 0)
                if b + 1 < B:
                    keys(b + 1, 0)
                attention_out(b, 1)
                if b + 1 < B:
                    keys(b + 1, 1)
            layer2_residual(B - 1)
            layer3_residual(B - 1, 0)
            layer3_residual(B - 1, 1)

        @block.tensor
        def _(pe):
            mm = nc.tensor.matmul

            def gammas(b):
                pe.wait_ge(S_par_in, 16)
                if b:
                    pe.wait_ge(S_demk_rdy, b)
                    pe.wait_ge(S_y_rdy, 2)
                mm(ps_q[:, 1, 0:P], cond_b[:, b], gbd_raw, start=True, stop=True).then_inc(S_gbd_ps, 1)
                pe.wait_ge(S_gbu_rdy, b)
                mm(ps_q[:, 0], cond_b[:, b], gbu_raw, start=True, stop=True).then_inc(S_gbu_ps, 1)

            def demodulation_k(b):
                if b:
                    pe.wait_ge(S_gbd_rdy, b + 1)
                pe.wait_ge(S_zeroed, 2)
                pe.wait_ge(S_pick_in, 16)
                pe.wait_ge(S_normk_rdy, 1)
                mm(ps_q[:, 1, P:P + D] if b else flat_a[1][:, 1, 0:D], pick[b], norm_k[:],
                   start=True, stop=True).then_inc(S_demk_ps, 1)

            def styles():
                pe.wait_ge(S_aff_in, 16)
                for l in range(MOD):
                    for c in range(NC_):
                        n = l * NC_ + c
                        last = mm(ps_p[:, 1, B * n:B * n + B], aff[:, l, P * c:P * c + P], cond, start=True, stop=True)
                last.then_inc(S_style_ps, 1)

            def variances_out():
                pe.wait_ge(S_squares, 2)
                pe.wait_ge(S_style_sq, 1)
                pe.wait_ge(S_gbd_rdy, 1)
                for i, l in enumerate((0, 2)):
                    for h in range(NC_):
                        for c in range(NC_):
                            at = AT_VAR + B * (NC_ * i + h)
                            last = mm(ps_q[:, 1, at:at + B], w_sq[:, l, c, P * h:P * h + P], style_sq[:, l, c],
                                      start=c == 0, stop=c == NC_ - 1)
                last.then_inc(S_varo_ps, 1)

            def variances_key():
                pe.wait_ge(S_squares, 1)
                pe.wait_ge(S_style_sq, 1)
                pe.wait_ge(S_gbu_rdy, 1)
                for c in range(NC_):
                    last = mm(ps_q[0:B, 0, 0:D], style_sq[:, 1, c], w_sq[:, 1, c], start=c == 0, stop=c == NC_ - 1)
                last.then_inc(S_vark_ps, 1)

            def down(b):
                pe.wait_ge(S_x_in, 16 * b + 16)
                pe.wait_ge(S_wdown_rdy, b + 1)
                if b >= 2:
                    pe.wait_ge(S_x2_rdy, 2 * (b - 1))
                for c in range(NC_):
                    for g in range(2):
                        last = mm(ps_p[HID * g:HID * g + HID, 0, 0:S // 2], w_down[:, c],
                                  x_sb[:, b, c, S // 2 * g:S // 2 * g + S // 2], start=c == 0, stop=c == NC_ - 1)
                last.then_inc(S_down_ps, 1)

            def up(b):
                pe.wait_ge(S_hid_rdy, 2 * b + 2)
                pe.wait_ge(S_wup_rdy, b + 1)
                if b == 0:
                    pe.wait_ge(S_styled, 6)
                for g in range(2):
                    for c in range(NC_):
                        last = mm(ps_p[:, g, S // 2 * c:S // 2 * c + S // 2], w_up[:, P * c:P * c + P],
                                  hid[:, g], start=True, stop=True)
                    last.then_inc(S_up_ps, 1)

            def layer1(b, h):
                pe.wait_ge(S_wl1_rdy, 2 * b + 2)
                pe.wait_ge(S_x0_rdy, 2 * b + 2)
                if b == 0:
                    pe.wait_ge(S_vark_in, 1)
                    if h:
                        pe.wait_ge(S_varo_in, 1)
                elif b == 1:
                    pe.wait_ge(S_demk_rdy, B)
                    pe.wait_ge(S_gbu_rdy, B)
                else:
                    pe.wait_ge(S_res_rdy, 2 * (b - 2) + h + 1)
                for c in range(NC_):
                    last = mm(ps_q[:, h], w_l1[:, c, P * h:P * h + P], x0[:, c], start=c == 0, stop=c == NC_ - 1)
                last.then_inc(S_l1_ps, 1)

            def keys(b, t, u):
                pe.wait_ge(S_wk_rdy, 2 * b + 2)
                for c in range(NC_):
                    pe.wait_ge(S_x1_rdy, 2 * b + c + 1)
                    at = TOK * t + P * u
                    last = mm(ps_p[:, t, D * u:D * u + D], x1[:, c, at:at + P], w_k[:, c],
                              start=c == 0, stop=c == NC_ - 1)
                if u == U - 1:
                    last.then_inc(S_k_ps, 1)

            def scores(b, t, first, end):
                n = 2 * b + t
                pe.wait_ge(S_kTz_rdy, 2 * n + 2)
                if b == 0:
                    pe.wait_ge(S_urow_rdy, 4)
                    pe.wait_ge(S_b3_rdy, t)
                pe.wait_ge(S_ot_rdy, max(n - 1, 0))
                for p in range(STRIP // 4 * first, STRIP // 4 * end):
                    for g in range(G):
                        r = slice(STRIP * g, STRIP * g + STRIP)
                        last = mm(ps_a[t][STRIP * g:STRIP * g + NH, p // PL, :, p % PL], kT[t][r, :, p],
                                  kTz[t][r, :, :, p], start=True, stop=True)
                if end == 4:
                    last.then_inc(S_s_ps, 1)

            def attend(b, t, first, end):
                n = 2 * b + t
                pe.wait_ge(S_pTz_rdy, 2 * n + 2)
                pe.wait_ge(S_vT_rdy, n + 1)
                pe.wait_ge(S_sc_rdy, n + 1)
                for p in range(STRIP // 4 * first, STRIP // 4 * end):
                    for g in range(G):
                        r = slice(STRIP * g, STRIP * g + STRIP)
                        last = mm(ps_a[t][STRIP * g:STRIP * g + HD, p // PL, :, p % PL], vT[t][r, :, p],
                                  pTz[t][r, :, :, p], start=True, stop=True)
                if end == 4:
                    last.then_inc(S_o_ps, 1)

            def transposes(b):
                pe.wait_ge(S_con_in, 16)
                pe.wait_ge(S_ot_rdy, 2 * b + 2)
                if b + 1 < B:
                    pe.wait_ge(S_y_rdy, 2 * b + 4)
                else:
                    pe.wait_ge(S_res_rdy, 2 * b)
                for h in range(NC_):
                    for t in range(TILES):
                        for u in range(U):
                            at = TOK * t + P * u
                            d = HD // NC_ * h
                            last = nc.tensor.transpose(ps_q[:, h, at:at + P],
                                                       ot[t][:, u, d:d + HD // NC_].rearrange("p d h -> p (d h)"), ident)
                    last.then_inc(S_tr_ps, 1)

            def layer2_out(b, c):
                pe.wait_ge(S_wo_rdy, 2 * b + c + 1)
                pe.wait_ge(S_att_rdy, 2 * b + c + 1)
                if b + 1 < B:
                    pe.wait_ge(S_kx_rdy, 2 * b + 4)
                for h in range(NC_):
                    last = mm(ps_p[:, h], w_o[:, c, P * h:P * h + P], att[:, c], start=c == 0, stop=c == NC_ - 1)
                    if c == NC_ - 1:
                        last.then_inc(S_op_ps, 1)

            def u_transposes():
                pe.wait_ge(S_u_added, 1)
                pe.wait_ge(S_att_rdy, 2)
                for c in range(NC_):
                    for b in range(B):
                        at = STRIP * (B * c + b)
                        last = nc.tensor.transpose(ps_q[:, 1, at:at + RANK], u_rows[:, b, P * c:P * c + P], ident[0:RANK, 0:RANK])
                last.then_inc(S_u_ps, 1)

            def layer3_down(b):
                pe.wait_ge(S_u_rdy, 1)
                pe.wait_ge(S_att_rdy, 2 * b + 2)
                for c in range(NC_):
                    pe.wait_ge(S_x2_rdy, 2 * b + c + 1)
                    for q in range(G):
                        last = mm(ps_q[STRIP * q:STRIP * q + STRIP, 0, 0:S // G], u_sb[:, c, b],
                                  x2[:, c, S // G * q:S // G * q + S // G], start=c == 0, stop=c == NC_ - 1)
                last.then_inc(S_xu_ps, 1)

            def layer3_up(b, h):
                pe.wait_ge(S_xu_rdy, b + 1)
                for q in range(G):
                    last = mm(ps_q[:, h, S // G * q:S // G * q + S // G], v_sb[:, q, P * h:P * h + P], xu[:], start=True, stop=True)
                last.then_inc(S_l3_ps, 1)

            def u_rows_product(n):
                pe.wait_ge(S_dec_in, 16 * (3 + G))
                pe.wait_ge(S_cond_pad, 1)
                pe.wait_ge(S_zeroed, 2)
                pe.wait_ge(S_demk_rdy, 1)
                for g in range(G):
                    j = G * n + g
                    bank = flat_a[n % 2][STRIP * g:STRIP * g + STRIP, n // 2]
                    if j < NCH:
                        last = mm(bank, cond_z[:], wdec_sb[:, 2 * j:2 * j + 2], start=True, stop=True)
                last.then_inc(S_urow_ps, 1)

            def layer3_bias_rows():
                pe.wait_ge(S_urow_rdy, 4)
                mm(flat_a[1][0:RANK, 0, AT_UB], wdecb_sb[:], cond, start=True, stop=True).then_inc(S_ub_ps, 1)

            def layer3_bias():
                pe.wait_ge(S_ub_added, 1)
                for h in range(NC_):
                    last = mm(flat_a[1][:, 0, AT_B3 + B * h:AT_B3 + B * h + B], v_sb[0:RANK, 0, P * h:P * h + P], ub_sb[:],
                              start=True, stop=True)
                last.then_inc(S_b3_ps, 1)

            styles()
            pe.wait_ge(S_cond_rep, 1)
            gammas(0)
            down(0)
            variances_key()
            up(0)
            variances_out()
            layer1(0, 0)
            demodulation_k(0)
            layer1(0, 1)
            keys(0, 0, 0)
            keys(0, 0, 1)
            keys(0, 1, 0)
            keys(0, 1, 1)
            gammas(1)
            demodulation_k(1)
            u_rows_product(0)
            u_rows_product(1)
            u_rows_product(2)
            u_rows_product(3)
            layer3_bias_rows()
            layer3_bias()
            for b in range(2, B):
                gammas(b)
                demodulation_k(b)

            for b in range(B):
                if b > 0:
                    transposes(b - 1)
                scores(b, 0, 0, 2)
                if b > 0:
                    layer2_out(b - 1, 0)
                scores(b, 0, 2, 3)
                if b == 1:
                    u_transposes()
                scores(b, 0, 3, 4)
                if b > 0:
                    layer2_out(b - 1, 1)
                scores(b, 1, 0, 2)
                if b > 0:
                    layer3_down(b - 1)
                if b + 1 < B:
                    down(b + 1)
                scores(b, 1, 2, 4)
                if b > 0:
                    layer3_up(b - 1, 0)
                if b + 1 < B:
                    up(b + 1)
                if b > 0:
                    layer3_up(b - 1, 1)
                attend(b, 0, 0, 2)
                if b + 1 < B:
                    layer1(b + 1, 0)
                attend(b, 0, 2, 4)
                if b + 1 < B:
                    layer1(b + 1, 1)
                attend(b, 1, 0, 2)
                if b + 1 < B:
                    keys(b + 1, 0, 0)
                    keys(b + 1, 0, 1)
                attend(b, 1, 2, 3)
                if b + 1 < B:
                    keys(b + 1, 1, 0)
                attend(b, 1, 3, 4)
                if b + 1 < B:
                    keys(b + 1, 1, 1)
            transposes(B - 1)
            layer2_out(B - 1, 0)
            layer2_out(B - 1, 1)
            layer3_down(B - 1)
            layer3_up(B - 1, 0)
            layer3_up(B - 1, 1)


def kernel(x, cond_512, L0_cond_down_project, L0_cond_down_gamma, L0_cond_down_beta,
           L0_cond_up_project, L0_cond_up_gamma, L0_cond_up_beta, L1_cond_weight, L1_cond_bias,
           L1_cond_affine_w, L1_cond_affine_b, L2_cond_k_aff_w, L2_cond_k_aff_b, L2_cond_k_w,
           L2_cond_k_b, L2_cond_o_aff_w, L2_cond_o_aff_b, L2_cond_o_w, L2_cond_o_b, L3_cond_W_dec,
           L3_cond_b_dec, L3_cond_V):
    import concourse.bacc as bacc
    from concourse.bass_utils import run_bass_kernel_spmd

    def halves(a):
        a = np.asarray(a).reshape(NC_, P, -1)
        return a.transpose(1, 0, 2).reshape(P, -1)

    def by_dim(a):
        a = np.asarray(a)
        return a.reshape((NH, HD) + a.shape[1:]).swapaxes(0, 1).reshape(a.shape)

    up = np.zeros((P, D), np.float32)
    for g in range(P // HID):
        up[HID * g:HID * g + HID] = np.asarray(L0_cond_up_project)
    params = np.concatenate(
        [np.asarray(cond_512).T]
        + [halves(a) for a in (L1_cond_affine_b, L2_cond_k_aff_b, by_dim(L2_cond_o_aff_b), L1_cond_bias, L2_cond_o_b)]
        + [np.asarray(a).T for a in (L1_cond_affine_w, L2_cond_k_aff_w, by_dim(L2_cond_o_aff_w))]
        + [halves(L0_cond_down_project)]
        + [np.asarray(a) for a in (L0_cond_down_gamma, L0_cond_down_beta, L0_cond_up_gamma, L0_cond_up_beta)]
        + [up], axis=1)
    weights = np.stack([halves(np.asarray(a).T) for a in (L1_cond_weight, L2_cond_k_w)]
                       + [halves(by_dim(np.asarray(L2_cond_o_w).T))], axis=1)
    wdec = np.asarray(L3_cond_W_dec).reshape(C, D + 1, RANK).transpose(0, 2, 1)
    eye = np.zeros((P, CONSTW), np.float32)
    eye[:, P:2 * P] = np.eye(P)
    picks = np.repeat(np.eye(B, dtype=np.float32), P, axis=1).reshape(B, B, P)
    for u in range(U):
        eye[:, 3 * P + u] = np.arange(P) % STRIP // (STRIP // U) == u
    arrays = {
        "xT": np.asarray(x).reshape(B, S, NC_, P).transpose(3, 0, 2, 1),
        "params": params,
        "weights": weights.reshape(P, MOD, NC_, D),
        "kb": np.asarray(L2_cond_k_b).reshape(1, D),
        "wdec": wdec[:, :, :D],
        "wdecb": wdec[:, :, D],
        "bdec": np.asarray(L3_cond_b_dec).reshape(D + 1, RANK).T,
        "vmat": np.asarray(L3_cond_V),
        "consts": eye,
        "picks": picks,
    }
    arrays = {k: np.ascontiguousarray(a) for k, a in arrays.items()}
    nc = bacc.Bacc("TRN2", target_bir_lowering=False, num_devices=1)
    args = [nc.dram_tensor(k, a.shape, mybir.dt.from_np(a.dtype), kind="ExternalInput").ap() for k, a in arrays.items()]
    out = nc.dram_tensor("outT", (P, B, NC_, S), mybir.dt.float32, kind="ExternalOutput").ap()
    cond_resid_kernel(nc, *args, out)
    r = run_bass_kernel_spmd(nc, [arrays], core_ids=[0])
    got = r.results[0]["outT"]
    return np.ascontiguousarray(got.transpose(1, 3, 2, 0).reshape(B, S, D))
```
